# Optimizing a Trainium2 kernel written in Bass

```python
import numpy as np
import jax
import jax.numpy as jnp

def _softmax(x, axis=-1):
    return jax.nn.softmax(x, axis=axis)
def _gelu(x):
    return jax.nn.gelu(x, approximate=True)
def _silu(x):
    return jax.nn.silu(x)
def _sigmoid(x):
    return jax.nn.sigmoid(x)
def _layernorm(x, axis=-1, eps=1e-5):
    m = jnp.mean(x, axis=axis, keepdims=True)
    v = jnp.var(x, axis=axis, keepdims=True)
    return (x - m) / jnp.sqrt(v + eps)
def _scatter_add(tgt, idx, src, axis=0):
    return tgt.at[idx].add(src)
def _segment_sum(src, seg, n):
    return jax.ops.segment_sum(src, seg, n)

kernel_name = 'mk_conv_attn_hybrid_d2_conv_nchw128_12ba79'

def setup_inputs(seed: int = 0):
    np.random.seed(seed)
    _w = jnp.asarray
    def _rec_inputs():
        import jax
        import jax.numpy as jnp
        _gk = jax.random.key(seed)
        x = -0.0005207 + 1.001 * jax.random.normal(jax.random.fold_in(_gk, 1), (4, 128, 64, 64), jnp.float32)
        return x
    x = _rec_inputs()
    def _L0_conv_setup():
        import jax, jax.numpy as jnp
        import numpy as np
        EPS = 1e-05
        GROUPS = 32

        def group_norm(x, w, b):
            B, C, H, W = x.shape
            g = x.reshape(B, GROUPS, C // GROUPS, H, W)
            mean = g.mean(axis=(2, 3, 4), keepdims=True)
            var = g.var(axis=(2, 3, 4), keepdims=True)
            g = (g - mean) * jax.lax.rsqrt(var + EPS)
            g = g.reshape(B, C, H, W)
            return g * w[None, :, None, None] + b[None, :, None, None]
        key = jax.random.key(seed)
        ks = jax.random.split(key, 8)
        B, C, H, W = (4, 128, 64, 64)
        s = 1.0 / np.sqrt(C)
        return {'x': jax.random.normal(ks[0], (B, C, H, W), jnp.float32), 'norm_w': jax.random.normal(ks[1], (C,), jnp.float32), 'norm_b': jax.random.normal(ks[2], (C,), jnp.float32), 'Wq': jax.random.normal(ks[3], (C, C), jnp.float32) * s, 'bq': jnp.zeros((C,), jnp.float32), 'Wk': jax.random.normal(ks[4], (C, C), jnp.float32) * s, 'bk': jnp.zeros((C,), jnp.float32), 'Wv': jax.random.normal(ks[5], (C, C), jnp.float32) * s, 'bv': jnp.zeros((C,), jnp.float32), 'Wo': jax.random.normal(ks[6], (C, C), jnp.float32) * s, 'bo': jnp.zeros((C,), jnp.float32)}
    _L0_conv_all = _L0_conv_setup()
    _L0_conv_in = {k: v for k, v in _L0_conv_all.items() if k in ('norm_w', 'norm_b', 'Wq', 'bq', 'Wk', 'bk', 'Wv', 'bv', 'Wo', 'bo', )}
    del _L0_conv_all

    def _L1_attn_setup():
        import jax, jax.numpy as jnp
        import numpy as np
        INPUT_DIM = 128
        HIDDEN_DIM = 128
        WINDOW_SIZE = 256
        BLOCK_SIZE = 256
        BATCH = 8
        SEQ = 8192
        key = jax.random.key(seed)
        ks = jax.random.split(key, 7)
        s = 1.0 / np.sqrt(INPUT_DIM)
        return {'x': jax.random.normal(ks[0], (BATCH, SEQ, INPUT_DIM), dtype=jnp.float32), 'Wq': jax.random.normal(ks[1], (HIDDEN_DIM, INPUT_DIM), dtype=jnp.float32) * s, 'bq': jax.random.normal(ks[2], (HIDDEN_DIM,), dtype=jnp.float32) * s, 'Wk': jax.random.normal(ks[3], (HIDDEN_DIM, INPUT_DIM), dtype=jnp.float32) * s, 'bk': jax.random.normal(ks[4], (HIDDEN_DIM,), dtype=jnp.float32) * s, 'Wv': jax.random.normal(ks[5], (HIDDEN_DIM, INPUT_DIM), dtype=jnp.float32) * s, 'bv': jax.random.normal(ks[6], (HIDDEN_DIM,), dtype=jnp.float32) * s}
    _L1_attn_all = _L1_attn_setup()
    _L1_attn_in = {k: v for k, v in _L1_attn_all.items() if k in ('Wq', 'bq', 'Wk', 'bk', 'Wv', 'bv', )}
    del _L1_attn_all

    def _L1_ffn_setup():
        import jax, jax.numpy as jnp
        import numpy as np
        B, N, D, C, E, K = (8, 8192, 128, 128, 8, 2)
        key = jax.random.key(seed)
        k0, k1, k2 = jax.random.split(key, 3)
        x = jax.random.normal(k0, (B, N, D), dtype=jnp.float32)
        router_w = jax.random.normal(k1, (D, E), dtype=jnp.float32) * 0.05
        router_b = jnp.zeros((E,), dtype=jnp.float32)
        expert_w = jax.random.normal(k2, (E, D, C), dtype=jnp.float32) * (1.0 / np.sqrt(D))
        expert_b = jnp.zeros((E, C), dtype=jnp.float32)
        return {'x': x, 'router_w': router_w, 'router_b': router_b, 'expert_w': expert_w, 'expert_b': expert_b}
    _L1_ffn_all = _L1_ffn_setup()
    _L1_ffn_in = {k: v for k, v in _L1_ffn_all.items() if k in ('router_w', 'router_b', 'expert_w', 'expert_b', )}
    del _L1_ffn_all

    return {
        "x": x,
        "L0_conv_norm_w": _L0_conv_in["norm_w"],
        "L0_conv_norm_b": _L0_conv_in["norm_b"],
        "L0_conv_Wq": _L0_conv_in["Wq"],
        "L0_conv_bq": _L0_conv_in["bq"],
        "L0_conv_Wk": _L0_conv_in["Wk"],
        "L0_conv_bk": _L0_conv_in["bk"],
        "L0_conv_Wv": _L0_conv_in["Wv"],
        "L0_conv_bv": _L0_conv_in["bv"],
        "L0_conv_Wo": _L0_conv_in["Wo"],
        "L0_conv_bo": _L0_conv_in["bo"],
        "L1_attn_Wq": _L1_attn_in["Wq"],
        "L1_attn_bq": _L1_attn_in["bq"],
        "L1_attn_Wk": _L1_attn_in["Wk"],
        "L1_attn_bk": _L1_attn_in["bk"],
        "L1_attn_Wv": _L1_attn_in["Wv"],
        "L1_attn_bv": _L1_attn_in["bv"],
        "L1_ffn_router_w": _L1_ffn_in["router_w"],
        "L1_ffn_router_b": _L1_ffn_in["router_b"],
        "L1_ffn_expert_w": _L1_ffn_in["expert_w"],
        "L1_ffn_expert_b": _L1_ffn_in["expert_b"],
    }

def reference(x, L0_conv_norm_w, L0_conv_norm_b, L0_conv_Wq, L0_conv_bq, L0_conv_Wk, L0_conv_bk, L0_conv_Wv, L0_conv_bv, L0_conv_Wo, L0_conv_bo, L1_attn_Wq, L1_attn_bq, L1_attn_Wk, L1_attn_bk, L1_attn_Wv, L1_attn_bv, L1_ffn_router_w, L1_ffn_router_b, L1_ffn_expert_w, L1_ffn_expert_b):
    import jax
    import jax.numpy as jnp
    def _L0_conv_ref(x, norm_w, norm_b, Wq, bq, Wk, bk, Wv, bv, Wo, bo):
        import jax, jax.numpy as jnp
        import numpy as np
        EPS = 1e-05
        GROUPS = 32

        def group_norm(x, w, b):
            B, C, H, W = x.shape
            g = x.reshape(B, GROUPS, C // GROUPS, H, W)
            mean = g.mean(axis=(2, 3, 4), keepdims=True)
            var = g.var(axis=(2, 3, 4), keepdims=True)
            g = (g - mean) * jax.lax.rsqrt(var + EPS)
            g = g.reshape(B, C, H, W)
            return g * w[None, :, None, None] + b[None, :, None, None]
        B, C, H, W = x.shape
        h = group_norm(x, norm_w, norm_b)
        h = h.transpose(0, 2, 3, 1)
        q = jnp.einsum('bhwc,cd->bhwd', h, Wq) + bq
        k = jnp.einsum('bhwc,cd->bhwd', h, Wk) + bk
        v = jnp.einsum('bhwc,cd->bhwd', h, Wv) + bv
        N = H * W
        qf = q.reshape(B, N, C)
        kf = k.reshape(B, N, C)
        vf = v.reshape(B, N, C)
        scores = jnp.einsum('bnc,bmc->bnm', qf, kf) * C ** (-0.5)
        attn = jax.nn.softmax(scores, axis=-1)
        o = jnp.einsum('bnm,bmc->bnc', attn, vf)
        o = jnp.einsum('bnc,cd->bnd', o, Wo) + bo
        o = o.reshape(B, H, W, C).transpose(0, 3, 1, 2)
        return x + o

    def _L1_attn_ref(x, Wq, bq, Wk, bk, Wv, bv):
        import jax, jax.numpy as jnp
        import numpy as np
        INPUT_DIM = 128
        HIDDEN_DIM = 128
        WINDOW_SIZE = 256
        BLOCK_SIZE = 256
        BATCH = 8
        SEQ = 8192
        B, S, D = x.shape
        bs, w = (BLOCK_SIZE, WINDOW_SIZE)
        nb = S // bs
        halo = w - 1
        W = bs + 2 * halo
        q = x @ Wq.T + bq
        k = x @ Wk.T + bk
        v = x @ Wv.T + bv
        k_pad = jnp.pad(k, ((0, 0), (halo, halo), (0, 0)))
        v_pad = jnp.pad(v, ((0, 0), (halo, halo), (0, 0)))
        starts = jnp.arange(nb) * bs
        idx = starts[:, None] + jnp.arange(W)[None, :]
        k_win = k_pad[:, idx, :]
        v_win = v_pad[:, idx, :]
        q_blk = q.reshape(B, nb, bs, -1)
        scale = 1.0 / jnp.sqrt(jnp.float32(D))
        attn = jnp.einsum('bnqh,bnkh->bnqk', q_blk, k_win) * scale
        out = jnp.einsum('bnqk,bnkh->bnqh', attn, v_win)
        return out.reshape(B, S, -1)

    def _L1_ffn_ref(x, router_w, router_b, expert_w, expert_b):
        import jax, jax.numpy as jnp
        import numpy as np
        B, N, D, C, E, K = (8, 8192, 128, 128, 8, 2)
        router_probs = jax.nn.softmax(x @ router_w + router_b, axis=-1)
        top_p, top_i = jax.lax.top_k(router_probs, K)
        top_p = top_p / jnp.sum(top_p, axis=-1, keepdims=True)
        expert_out = jnp.einsum('bnd,edc->bnec', x, expert_w) + expert_b
        gathered = jnp.take_along_axis(expert_out, top_i[..., None], axis=2)
        return jnp.einsum('bnk,bnkc->bnc', top_p, gathered)

    def _gn(v, G=32, eps=1e-5):
        B_, C_, H_, W_ = v.shape
        g = v.reshape(B_, G, C_ // G, H_, W_)
        m = jnp.mean(g, axis=(2, 3, 4), keepdims=True)
        s = jnp.var(g, axis=(2, 3, 4), keepdims=True)
        return ((g - m) / jnp.sqrt(s + eps)).reshape(v.shape)

    def _ln_c(v, eps=1e-6):
        m = jnp.mean(v, axis=1, keepdims=True)
        s = jnp.var(v, axis=1, keepdims=True)
        return (v - m) / jnp.sqrt(s + eps)

    def _ln_t(v, eps=1e-5):
        m = jnp.mean(v, axis=-1, keepdims=True)
        s = jnp.var(v, axis=-1, keepdims=True)
        return (v - m) / jnp.sqrt(s + eps)

    def _to_tokens(v):
        B_, C_, H_, W_ = v.shape
        return v.reshape(B_, C_, H_ * W_).transpose(0, 2, 1)
    def _from_tokens(t, like):
        B_, C_, H_, W_ = like.shape
        return t.transpose(0, 2, 1).reshape(B_, C_, H_, W_)

    x = _L0_conv_ref(x, L0_conv_norm_w, L0_conv_norm_b, L0_conv_Wq, L0_conv_bq, L0_conv_Wk, L0_conv_bk, L0_conv_Wv, L0_conv_bv, L0_conv_Wo, L0_conv_bo)
    t = _to_tokens(x)
    t = t + _L1_attn_ref(_ln_t(t), L1_attn_Wq, L1_attn_bq, L1_attn_Wk, L1_attn_bk, L1_attn_Wv, L1_attn_bv)
    t = t + _L1_ffn_ref(_ln_t(t), L1_ffn_router_w, L1_ffn_router_b, L1_ffn_expert_w, L1_ffn_expert_b)
    x = _from_tokens(t, x)
    return x


_drawn_inputs = setup_inputs


def setup_inputs(seed=0):
    import zlib

    import numpy as np

    out = dict(_drawn_inputs(seed))
    spreads = {'L0_conv_bq': (0.0, 0.1),
     'L0_conv_bk': (0.0, 2.0),
     'L0_conv_bv': (0.0, 0.1),
     'L0_conv_bo': (0.0, 0.1),
     'L1_ffn_router_b': (0.0, 2.0),
     'L1_ffn_expert_b': (0.0, 2.0)}
    factors = {'L1_ffn_router_w': 24.708, 'L1_ffn_expert_w': 8.0}
    for name, (base, spread) in spreads.items():
        noise = np.random.default_rng([zlib.crc32(name.encode()), seed]).standard_normal(out[name].shape)
        drawn = base * np.exp(spread * noise) if base else spread * noise
        out[name] = jnp.asarray(drawn.astype(out[name].dtype))
    for name, factor in factors.items():
        out[name] = (out[name] * factor).astype(out[name].dtype)
    return out
```

```python
import concourse.bass as bass
from concourse import mybir
from contextlib import ExitStack



def conv_attn_hybrid_kernel(nc, x, norm_w, norm_b, wq, bq, wk, bk, wv, bv_rows, wo, bo,
                            l1_wqT, l1_bq, l1_wkvT, l1_bkv_rows, router_w, router_b_rows,
                            expert_w, expert_b3, c_ident, c_center, c_mean, c_group, c_sel, c_lower,
                            c_notlast, out):
    fp32, bf16, fp16, i32 = mybir.dt.float32, mybir.dt.bfloat16, mybir.dt.float16, mybir.dt.int32
    ALU = mybir.AluOpType
    ACT = mybir.ActivationFunctionType
    AX = mybir.AxisListType

    B, C, N = x.shape
    P = 128
    T = 512
    NCH = N // T
    KT = N // P
    NP = KT // 2
    E = router_w.shape[1]
    GPARTS = 3
    NB = N // 256
    GN_EPS = LN_EPS = 1e-5
    TOP = 16384.0
    RSQRT_SEED = float(0x5F3759DF)
    RSQRT_STEPS = 12
    PREP_STEPS = 27
    H_STEP = 21
    GATE_STEPS = 15

    ctx = ExitStack()
    with ctx:
        def sb(name, shape, dt=fp32):
            return ctx.enter_context(nc.sbuf_tensor(name, shape, dt))

        def pb(name, shape):
            return ctx.enter_context(nc.psum_tensor(name, shape, fp32))

        def sem(name):
            return ctx.enter_context(nc.semaphore(name))

        ident = sb("ident", [P, P])
        identb = sb("identb", [P, P], bf16)
        center = sb("center", [P, P])
        meancol = sb("meancol", [P, 1])
        group = sb("group", [P, P])
        ones = sb("ones", [P, P])
        sel = sb("sel", [E * GPARTS, E, P], bf16)
        lower = sb("lower", [P, E * E])
        notlast = sb("notlast", [P, 1])
        wq_s, wk_s, wv_s, wo_s = (sb(n, [P, P]) for n in ("wq_s", "wk_s", "wv_s", "wo_s"))
        wq1_s = sb("wq1_s", [P, P])
        wkv1_s = sb("wkv1_s", [P, 2 * P])
        cols = sb("cols", [P, 6])
        gw_c, gb_c, bq_c, bk_c, bo_c, bq1_c = (cols[:, i:i + 1] for i in range(6))
        bv_s = sb("bv_s", [P, P])
        bkv1_s = sb("bkv1_s", [P, 2 * P])
        rw_s = sb("rw_s", [P, E])
        rb_s = sb("rb_s", [P, E])
        ew_s = sb("ew_s", [P, E, P])
        eb_s = sb("eb_s", [E * GPARTS, P])

        xs = sb("xs", [P, N])
        qh, ql, kh, kl = (sb(n, [P, N], fp16) for n in ("qh", "ql", "kh", "kl"))
        vs = sb("vs", [P, KT, P])
        st = sb("st", [P, NP, 2 * T])
        self32 = st[0:E * GPARTS, NP - 1, 0:E * P]
        temps = st[:, :, :].rearrange("p a n -> p (a n)")
        h = temps[:, 0:N]
        qf, kf = temps[:, N:2 * N], temps[:, 2 * N:3 * N]
        qkf = temps[:, N:3 * N].rearrange("p (a n) -> p a n", a=2)
        bstats = sb("bstats", [P, NCH, 6])
        chst = sb("chst", [P, 2])
        gst = sb("gst", [P, 2])
        gsm = sb("gsm", [P, 8])
        amx = sb("amx", [P, 2, NCH])
        am2 = sb("am2", [P, 2])
        amr = sb("amr", [2, 1])
        amd = sb("amd", [2, 2])
        ag = sb("ag", [P, 2])
        iv = sb("iv", [P, 2])
        sc = sb("sc", [P, 1])

        acc = sb("acc", [P, 2 * T])
        mx = sb("mx", [P, T])
        mq = sb("mq", [P, 4])
        dgm = sb("dgm", [P, 4, P])
        rs = sb("rs", [P, 2 * T])
        rl = sb("rl", [P, 4])
        dgl = sb("dgl", [P, 4, P])
        osb = sb("osb", [P, T])

        tt = sb("tt", [P, 2, T])
        xc = sb("xc", [P, T])
        sq = sb("sq", [P, T])
        rsm = [sb(f"rsm{k}", [P, 4, 4]) for k in range(2)]
        dgn = sb("dgn", [P, 4, P])
        y = sb("y", [P, T])
        q1 = sb("q1", [P, 2, T])
        k3 = sb("k3", [P, 4, P])
        v3 = sb("v3", [P, 4, 3, P])
        mst = sb("mst", [P, (NB + 2) * P])
        mcur = sb("mcur", [P, 2, P])
        t1 = sb("t1", [P, T])
        lg, ex, em, gt, gr = (sb(n, [P, 4, E]) for n in ("lg", "ex", "em", "gt", "gr"))
        lm, es, er = (sb(n, [P, 4]) for n in ("lm", "es", "er"))
        above, equal = (sb(n, [P, 4, E * E]) for n in ("above", "equal"))
        rank = sb("rank", [P, 4, E])
        g24 = sb("g24", [P, 4, GPARTS * E], bf16)
        gT = sb("gT", [GPARTS * E, T], bf16)
        gTf = dgn[0:GPARTS * E, :, :].rearrange("p a n -> p (a n)")
        zg = sb("zg", [P, 2, T])
        ob = sb("ob", [P, 2, T])

        psS = pb("psS", [P, 2, 2 * T])
        psM = pb("psM", [P, T])
        psO = pb("psO", [P, T])
        ps0 = pb("ps0", [P, T])
        ps1 = pb("ps1", [P, T])

        consts_loaded, consts_made, x_loaded = sem("consts_loaded"), sem("consts_made"), sem("x_loaded")
        prep_step, group_summed, h_read = sem("prep_step"), sem("group_summed"), sem("h_read")
        q_made, kv_made = sem("q_made"), sem("kv_made")
        q_stored, kv_held, absmax_taken, absmax_turned = (
            sem(n) for n in ("q_stored", "kv_held", "absmax_taken", "absmax_turned"))
        absmax_shared, high_parts, low_parts = sem("absmax_shared"), sem("high_parts"), sem("low_parts")
        scores_ready, scores_copied, max_taken, shifted = (
            sem(n) for n in ("scores_ready", "scores_copied", "max_taken", "shifted"))
        probs_ready, pv_done, rows_added = sem("probs_ready"), sem("pv_done"), sem("rows_added")
        max_folded, max_turned, query_max, max_diag, max_spread = (
            sem(n) for n in ("max_folded", "max_turned", "query_max", "max_diag", "max_spread"))
        sums_ready, sums_inverted, sums_diag, sums_spread = (
            sem(n) for n in ("sums_ready", "sums_inverted", "sums_diag", "sums_spread"))
        heads_copied, heads_normed, heads_mixed, layer0_out = (
            sem(n) for n in ("heads_copied", "heads_normed", "heads_mixed", "layer0_out"))
        centered, center_copied, squared, var_ready, rsqrt_step, ln_diag, ln_spread, normed = (
            [sem(f"{n}{k}") for k in range(2)] for n in
            ("centered", "center_copied", "squared", "var_ready", "rsqrt_step", "ln_diag", "ln_spread", "normed"))
        l1_q_made, l1_q_stored, l1_kv_made, l1_kv_stored, edges_masked, block_summed, window_added = (
            sem(n) for n in ("l1_q_made", "l1_q_stored", "l1_kv_made", "l1_kv_stored", "edges_masked",
                             "block_summed", "window_added"))
        window_scaled, attended, t1_ready, logits_made, gate_step, exps_made = (
            sem(n) for n in ("window_scaled", "attended", "t1_ready", "logits_made", "gate_step", "exps_made"))
        gates_turned, gates_stored, gate_spread, gated, expert_done, result_ready, stored = (
            sem(n) for n in ("gates_turned", "gates_stored", "gate_spread", "gated", "expert_done",
                             "result_ready", "stored"))

        block = ctx.enter_context(nc.Block())

        n_const = [0]

        def walk(eng, prepare, first_scores, chunk, finish):
            def image(b, n0, first):
                prepare(b, n0)
                first_scores(b, n0)
                chunk(b, 0, n0, 0, 2, not first, not first)
                chunk(b, 1, n0 + 1, 1, 2, True, not first)
                if first:
                    for c in range(2, NCH - 2):
                        chunk(b, c, n0 + c, c % 2, 2, True, True)
                else:
                    with eng.Fori(1, NCH // 2 - 1) as twos:
                        c = twos * 2
                        chunk(b, c, n0 + c, 0, 2, True, True)
                        chunk(b, c + 1, n0 + c + 1, 1, 2, True, True)
                chunk(b, NCH - 2, n0 + NCH - 2, 0, 1, True, True)
                chunk(b, NCH - 1, n0 + NCH - 1, 1, 0, True, True)
            image(0, 0, True)
            with eng.Fori(1, B) as b:
                image(b, b * NCH, False)
            finish()

        def tile_in_image(c, back):
            return (c - back) % NCH if isinstance(c, int) else c - back

        @block.sync
        def _(sp):
            def const(dst, src):
                sp.dma_start(dst, src).then_inc(consts_loaded, 16)
                n_const[0] += 16
            for i, v in enumerate((norm_w, norm_b, bq, bk, bo, l1_bq)):
                const(cols[:, i:i + 1], v)
            for dst, src in ((group, c_group), (wq_s, wq), (wk_s, wk), (wv_s, wv), (bv_s, bv_rows)):
                const(dst[:, :], src)

            def load_x(b):
                sp.dma_start(xs[:, :], x[bass.ds(b, 1), :, :].rearrange("a c n -> (a c) n")).then_inc(x_loaded, 16)

            def store(m, b, j):
                sp.wait_ge(result_ready, m + 1)
                par = store.par
                sp.dma_start(out[bass.ds(b, 1), :, bass.ds(j * T, T)].rearrange("a c n -> (a c) n"),
                             ob[:, par, :]).then_inc(stored, 16)

            def prepare(b, n0):
                if isinstance(b, int):
                    load_x(b)
                    for dst, src in ((ident, c_ident), (center, c_center), (wo_s, wo),
                                     (self32, c_sel), (lower, c_lower), (wq1_s, l1_wqT), (wkv1_s, l1_wkvT),
                                     (bkv1_s, l1_bkv_rows), (rw_s, router_w), (rb_s, router_b_rows),
                                     (eb_s, expert_b3), (notlast, c_notlast), (meancol, c_mean)):
                        const(dst if dst is self32 else dst[:, :], src)
                    const(ew_s[:, :, :], expert_w.rearrange("e d c -> d e c"))
                else:
                    sp.wait_ge(layer0_out, n0)
                    load_x(b)

            def chunk(b, c, n, par, ahead, first_half, second_half):
                if second_half:
                    store.par = par
                    crossed = isinstance(c, int) and c < 2
                    store(n - 2, b - 1 if crossed else b, tile_in_image(c, 2))

            def finish():
                for m in (B * NCH - 2, B * NCH - 1):
                    store.par = m % 2
                    store(m, m // NCH, m % NCH)
                sp.wait_ge(stored, 16 * B * NCH)

            walk(sp, prepare, lambda b, n0: None, chunk, finish)

        CONSTS = n_const[0]

        @block.gpsimd
        def _(pool):
            nc.gpsimd.memset(ones[:, :], 1.0).then_inc(consts_made, 1)

            def ln_diagonal(k, m):
                pool.wait_ge(rsqrt_step[k], RSQRT_STEPS * m + RSQRT_STEPS)
                if not (isinstance(m, int) and m == 0):
                    pool.wait_ge(ln_spread[k], m)
                nc.gpsimd.tensor_tensor(dgn[:, :, :], ident[:, :].unsqueeze(1).to_broadcast([P, 4, P]),
                                        rsm[k][:, 3, :].unsqueeze(2).to_broadcast([P, 4, P]),
                                        ALU.mult).then_inc(ln_diag[k], 1)

            def add_rows(n, j):
                pool.wait_ge(probs_ready, NP * n + j + 1)
                if j == 1:
                    if not (isinstance(n, int) and n == 0):
                        pool.wait_ge(sums_ready, n)
                    a = st[:, 0, :]
                else:
                    pool.wait_ge(rows_added, (NP - 1) * n + j - 1)
                    a = rs[:, :]
                nc.gpsimd.tensor_tensor(rs[:, :], a, st[:, j, :], ALU.add).then_inc(rows_added, 1)

            def chunk(b, c, n, par, ahead, first_half, second_half):
                for j in range(NP):
                    if j:
                        add_rows(n, j)
                    if first_half and j == 3:
                        ln_diagonal(0, n - 1)
                    if second_half and j == 9:
                        ln_diagonal(1, n - 2)

            def finish():
                ln_diagonal(0, B * NCH - 1)
                ln_diagonal(1, B * NCH - 2)
                ln_diagonal(1, B * NCH - 1)

            pool.wait_ge(consts_loaded, CONSTS)
            walk(pool, lambda b, n0: None, lambda b, n0: None, chunk, finish)

        @block.scalar
        def _(act):
            act.wait_ge(consts_loaded, CONSTS)
            nc.scalar.activation(sel[:, :, :].rearrange("p a n -> p (a n)"), self32, ACT.Copy).then_inc(consts_made, 1)
            nc.scalar.activation(identb[:, :], ident[:, :], ACT.Copy).then_inc(consts_made, 1)

            def prepare(b, n0):
                for t in range(NCH):
                    act.wait_ge(q_made, NCH * b + t + 1)
                    nc.scalar.activation(qf[:, t * T:(t + 1) * T], psS[:, t % 2, 0:T], ACT.Identity,
                                         bias=bq_c).then_inc(q_stored, 1)
                act.wait_ge(prep_step, PREP_STEPS * b + PREP_STEPS)
                for dst, src, s in ((kh, kf, 1), (qh, qf, 0)):
                    nc.scalar.activation(dst[:, :], src, ACT.Copy, scale=iv[:, s:s + 1]).then_inc(high_parts, 1)

            def copy_scores(n, j, first):
                act.wait_ge(scores_ready, NP * n + j + 1)
                if not first:
                    act.wait_ge(pv_done, NP * (n - 1) + j + 1)
                    act.wait_ge(rows_added, (NP - 1) * (n - 1) + max(j, 1))
                nc.scalar.activation(st[:, j, :], psS[:, j % 2, :], ACT.Copy).then_inc(scores_copied, 1)

            def exponentiate(n, j):
                act.wait_ge(shifted, NP * n + j + 1)
                nc.scalar.activation(st[:, j, :], st[:, j, :], ACT.Exp, scale=sc[:, :]).then_inc(probs_ready, 1)

            def first_scores(b, n0):
                act.wait_ge(low_parts, 2 * b + 2)
                for j in range(NP):
                    copy_scores(n0, j, True)

            def ln_center(k, m):
                act.wait_ge(centered[k], m + 1)
                nc.scalar.activation(xc[:, :], ps0[:, :], ACT.Copy).then_inc(center_copied[k], 1)
                act.wait_ge(center_copied[k], m + 1)
                nc.scalar.activation(sq[:, :], xc[:, :], ACT.Square).then_inc(squared[k], 1)

            def l1_query(m, par):
                act.wait_ge(l1_q_made, m + 1)
                nc.scalar.activation(q1[:, par, :], ps1[:, :], ACT.Identity, bias=bq1_c).then_inc(l1_q_stored, 1)

            def scale_window(m, j, tiles_added):
                act.wait_ge(window_added, 4 * tiles_added)
                nc.scalar.activation(mcur[:, :, :].rearrange("p a n -> p (a n)"),
                                     mst[:, bass.ds((2 * j + 1) * P, 2 * P)], ACT.Copy,
                                     scale=float(C) ** -0.5).then_inc(window_scaled, 1)

            def exp_logits(m):
                act.wait_ge(gate_step, GATE_STEPS * m + 3)
                nc.scalar.activation(ex[:, :, :], em[:, :, :], ACT.Exp).then_inc(exps_made, 1)

            def store_gates(m):
                act.wait_ge(gates_turned, m + 1)
                nc.scalar.activation(gT[:, :], ps0[0:GPARTS * E, 0:T // 2].bitcast(bf16), ACT.Copy).then_inc(gates_stored, 1)
                act.wait_ge(gates_stored, 2 * m + 1)
                nc.scalar.activation(gTf, gT[:, :], ACT.Copy).then_inc(gates_stored, 1)

            def copy_heads(n):
                act.wait_ge(pv_done, NP * n + NP)
                nc.scalar.activation(osb[:, :], psO[:, :], ACT.Copy).then_inc(heads_copied, 1)

            def chunk(b, c, n, par, ahead, first_half, second_half):
                for j in range(3):
                    exponentiate(n, j)
                for j in range(NP):
                    if ahead:
                        copy_scores(n + 1, j, False)
                    if j + 3 < NP:
                        exponentiate(n, j + 3)
                    if first_half:
                        if j == 1:
                            ln_center(0, n - 1)
                        if j == 4:
                            l1_query(n - 1, 1 - par)
                    if second_half:
                        if j == 6:
                            scale_window(n - 2, tile_in_image(c, 2), n)
                        if j == 8:
                            ln_center(1, n - 2)
                        if j == 11:
                            exp_logits(n - 2)
                        if j == 12:
                            store_gates(n - 2)
                copy_heads(n)

            def finish():
                last = B * NCH
                ln_center(0, last - 1)
                l1_query(last - 1, 1)
                for m in (last - 2, last - 1):
                    scale_window(m, m % NCH, last)
                    ln_center(1, m)
                    exp_logits(m)
                    store_gates(m)

            walk(act, prepare, first_scores, chunk, finish)

        @block.vector
        def _(dve):
            v = nc.vector
            dve.wait_ge(consts_loaded, CONSTS)

            def rsqrt(var, s, step, base, k0):
                def link(ins):
                    ins.then_inc(step, 1)
                    link.k += 1
                    dve.wait_ge(step, base + link.k)
                link.k = k0
                link(v.tensor_scalar(s[1].bitcast(i32), s[0].bitcast(i32), 1, None, ALU.logical_shift_right))
                link(v.tensor_scalar(s[3].bitcast(i32), s[1].bitcast(i32), -1.0, RSQRT_SEED, ALU.mult, ALU.add))
                for _ in range(3):
                    link(v.tensor_tensor(s[1], s[3], s[3], ALU.mult))
                    link(v.scalar_tensor_tensor(s[2], s[1], -0.5, s[0], ALU.mult, ALU.mult))
                    link(v.scalar_tensor_tensor(s[3], s[2], 1.5, s[3], ALU.add, ALU.mult))
                return link.k

            def prepare(b, n0):
                base = PREP_STEPS * b
                k = 0

                def link(ins):
                    nonlocal k
                    ins.then_inc(prep_step, 1)
                    k += 1
                    dve.wait_ge(prep_step, base + k)

                dve.wait_ge(x_loaded, 16 * b + 16)
                for t in range(NCH):
                    last = v.bn_stats(bstats[:, t, :], xs[:, t * T:(t + 1) * T])
                if not isinstance(b, int):
                    dve.wait_ge(window_scaled, n0 - 2)
                link(last)
                v.memset(mst[:, 0:2 * P], 0.0).then_inc(prep_step, 1)
                k += 1
                link(v.bn_aggr(chst[:, :], bstats[:, :, :].rearrange("p a n -> p (a n)")))
                link(v.scalar_tensor_tensor(chst[:, 1:2], chst[:, 0:1], chst[:, 0:1], chst[:, 1:2], ALU.mult, ALU.add))
                dve.wait_ge(group_summed, b + 1)
                link(v.tensor_copy(gst[:, :], ps0[:, 0:2]))
                s = [gsm[:, i:i + 1] for i in range(8)]
                link(v.scalar_tensor_tensor(s[4], gst[:, 0:1], gst[:, 0:1], gst[:, 1:2], ALU.mult, ALU.subtract))
                link(v.tensor_scalar(s[0], s[4], -1.0, GN_EPS, ALU.mult, ALU.add))
                k = rsqrt(None, s, prep_step, base, k)
                link(v.tensor_tensor(s[5], s[3], gw_c, ALU.mult))
                link(v.scalar_tensor_tensor(s[6], gst[:, 0:1], s[5], gb_c, ALU.mult, ALU.subtract))
                if not isinstance(b, int):
                    dve.wait_ge(pv_done, NP * n0)
                    dve.wait_ge(rows_added, (NP - 1) * n0)
                link(v.tensor_scalar(h, xs[:, :], s[5], s[6], ALU.mult, ALU.subtract))
                for t in range(NCH):
                    i = NCH * b + t
                    tile = slice(t * T, (t + 1) * T)
                    dve.wait_ge(kv_made, i + 1)
                    v.tensor_scalar(kf[:, tile], psS[:, t % 2, T:2 * T], bk_c, None, ALU.add).then_inc(kv_held, 1)
                    v.tensor_tensor(vs[:, 4 * t:4 * t + 4, :], (ps0, ps1)[t % 2][:, :].rearrange("p (a n) -> p a n", a=4),
                                    bv_s[:, :].unsqueeze(1).to_broadcast([P, 4, P]), ALU.add).then_inc(kv_held, 1)
                    dve.wait_ge(q_stored, i + 1)
                    dve.wait_ge(kv_held, 2 * i + 2)
                    last = v.tensor_reduce(amx[:, :, t:t + 1], qkf[:, :, tile], AX.X, ALU.max,
                                           apply_absolute_value=True)
                link(last)
                v.tensor_reduce(am2[:, :].unsqueeze(2), amx[:, :, :], AX.X, ALU.max).then_inc(absmax_taken, 1)
                dve.wait_ge(absmax_turned, b + 1)
                link(v.tensor_reduce(amr[:, :], ps0[0:2, 0:P], AX.X, ALU.max))
                v.tensor_scalar(amd[:, :], ident[0:2, 0:2], amr[:, :], None, ALU.mult).then_inc(prep_step, 1)
                k += 1
                dve.wait_ge(absmax_shared, b + 1)
                link(v.tensor_scalar(ag[:, :], ps0[:, 0:2], 1e-30, None, ALU.max))
                v.tensor_scalar(sc[:, :], ag[:, 0:1], ag[:, 1:2], float(C) ** -0.5 / TOP ** 2, ALU.mult, ALU.mult)
                link(v.reciprocal(iv[:, :], ag[:, :]))
                v.tensor_scalar(iv[:, :], iv[:, :], TOP, None, ALU.mult).then_inc(prep_step, 1)
                k += 1
                assert k == PREP_STEPS, k
                dve.wait_ge(prep_step, base + PREP_STEPS)
                for i, (lo, hi, src, s) in enumerate(((kl, kh, kf, 1), (ql, qh, qf, 0))):
                    dve.wait_ge(high_parts, 2 * b + i + 1)
                    v.scalar_tensor_tensor(lo[:, :], src, iv[:, s:s + 1], hi[:, :], ALU.mult,
                                           ALU.subtract).then_inc(low_parts, 1)

            def take_max(n, j):
                dve.wait_ge(scores_copied, NP * n + j + 1)
                if j == 0:
                    v.tensor_copy(acc[:, :], psS[:, 0, :]).then_inc(max_taken, 1)
                else:
                    dve.wait_ge(max_taken, NP * n + j)
                    v.tensor_tensor(acc[:, :], psS[:, j % 2, :], acc[:, :], ALU.max).then_inc(max_taken, 1)

            def fold_max(n):
                dve.wait_ge(max_taken, NP * n + NP)
                v.tensor_tensor(mx[:, :], acc[:, 0:T], acc[:, T:2 * T], ALU.max).then_inc(max_folded, 1)

            def diagonal(dst, col):
                return v.tensor_tensor(dst[:, :, :], ident[:, :].unsqueeze(1).to_broadcast([P, 4, P]),
                                       col.unsqueeze(2).to_broadcast([P, 4, P]), ALU.mult)

            def query_maxima(n):
                dve.wait_ge(max_turned, n + 1)
                v.tensor_reduce(mq[:, :].unsqueeze(2), ps1[:, :].rearrange("p (a n) -> p a n", a=4), AX.X,
                                ALU.max).then_inc(query_max, 1)
                dve.wait_ge(query_max, n + 1)
                if not (isinstance(n, int) and n == 0):
                    dve.wait_ge(max_spread, n)
                diagonal(dgm, mq[:, :]).then_inc(max_diag, 1)

            def invert_sums(n):
                dve.wait_ge(sums_ready, n + 1)
                v.reciprocal(rl[:, :], ps0[:, 0:4]).then_inc(sums_inverted, 1)
                dve.wait_ge(sums_inverted, n + 1)
                if not (isinstance(n, int) and n == 0):
                    dve.wait_ge(sums_spread, n)
                diagonal(dgl, rl[:, :]).then_inc(sums_diag, 1)

            def norm_heads(n):
                dve.wait_ge(sums_spread, n + 1)
                dve.wait_ge(heads_copied, n + 1)
                v.tensor_tensor(osb[:, :], ps0[:, :], osb[:, :], ALU.mult).then_inc(heads_normed, 1)

            def residual(c, n, par):
                dve.wait_ge(heads_mixed, n + 1)
                v.scalar_tensor_tensor(tt[:, par, :], ps1[:, :], bo_c, xs[:, bass.ds(c * T, T)], ALU.add,
                                       ALU.add).then_inc(layer0_out, 1)

            def shift(n, j):
                if j == 0:
                    dve.wait_ge(max_spread, n + 1)
                pair = st[:, j, :].rearrange("p (a n) -> p a n", a=2)
                v.tensor_tensor(pair, pair, psM[:, :].unsqueeze(1).to_broadcast([P, 2, T]),
                                ALU.subtract).then_inc(shifted, 1)

            def first_scores(b, n0):
                for j in range(NP):
                    take_max(n0, j)
                fold_max(n0)
                query_maxima(n0)

            def ln_rsqrt(k, m):
                dve.wait_ge(var_ready[k], m + 1)
                s = [rsm[k][:, i, :] for i in range(4)]
                base = RSQRT_STEPS * m
                v.tensor_scalar(s[0], ps0[:, 0:4], LN_EPS, None, ALU.add).then_inc(rsqrt_step[k], 1)
                dve.wait_ge(rsqrt_step[k], base + 1)
                assert rsqrt(None, s, rsqrt_step[k], base, 1) == RSQRT_STEPS

            def ln_scale(k, m):
                dve.wait_ge(ln_spread[k], m + 1)
                v.tensor_tensor(y[:, :], ps0[:, :], xc[:, :], ALU.mult).then_inc(normed[k], 1)

            def l1_keys_values(m):
                for i, bank in enumerate((ps0, ps1)):
                    dve.wait_ge(l1_kv_made, 2 * m + i + 1)
                    kv = bank[:, :].rearrange("p (a n) -> p a n", a=2)
                    v.tensor_tensor(k3[:, 2 * i:2 * i + 2, :], kv[:, :, 0:P],
                                    bkv1_s[:, 0:P].unsqueeze(1).to_broadcast([P, 2, P]), ALU.add)
                    for s in range(3):
                        last = v.tensor_tensor(v3[:, 2 * i:2 * i + 2, s, :], kv[:, :, P:2 * P],
                                               bkv1_s[:, P:2 * P].unsqueeze(1).to_broadcast([P, 2, P]), ALU.add)
                    last.then_inc(l1_kv_stored, 1)
                dve.wait_ge(l1_kv_stored, 2 * m + 2)
                for i in (0, 2):
                    v.memset(v3[0:1, i, 2, :], 0.0)
                for i in (1, 3):
                    last = v.tensor_scalar(v3[:, i, 0, :], v3[:, i, 1, :], notlast[:, :], None, ALU.mult)
                last.then_inc(edges_masked, 1)

            def add_windows(m, j):
                for i, bank in enumerate((ps0, ps1)):
                    dve.wait_ge(block_summed, 2 * m + i + 1)
                    if i:
                        dve.wait_ge(window_added, 4 * m + 2)
                    slot = (2 * j + i) * P
                    have = mst[:, bass.ds(slot, 2 * P)]
                    v.tensor_tensor(have, bank[:, 0:2 * P], have, ALU.add).then_inc(window_added, 1)
                    v.tensor_copy(mst[:, bass.ds(slot + 2 * P, P)], bank[:, 2 * P:3 * P]).then_inc(window_added, 1)

            def l1_residual(m, par):
                dve.wait_ge(attended, m + 1)
                if not (isinstance(m, int) and m == 0):
                    dve.wait_ge(result_ready, m)
                v.tensor_tensor(t1[:, :], ps0[:, :], tt[:, par, :], ALU.add).then_inc(t1_ready, 1)

            def gate_chain(m, k0):
                def link(ins):
                    ins.then_inc(gate_step, 1)
                    link.k += 1
                    dve.wait_ge(gate_step, GATE_STEPS * m + link.k)
                link.k = k0
                return link

            def gate_logits(m):
                dve.wait_ge(logits_made, m + 1)
                link = gate_chain(m, 0)
                link(v.tensor_tensor(lg[:, :, :], ps0[:, 0:4 * E].rearrange("p (a n) -> p a n", a=4),
                                     rb_s[:, :].unsqueeze(1).to_broadcast([P, 4, E]), ALU.add))
                link(v.tensor_reduce(lm[:, :].unsqueeze(2), lg[:, :, :], AX.X, ALU.max))
                link(v.tensor_tensor(em[:, :, :], lg[:, :, :], lm[:, :].unsqueeze(2).to_broadcast([P, 4, E]),
                                     ALU.subtract))
                for u in range(4):
                    one = lg[:, u, :]
                    other, own = one.unsqueeze(1).to_broadcast([P, E, E]), one.unsqueeze(2).to_broadcast([P, E, E])
                    v.tensor_tensor(above[:, u, :].rearrange("p (a n) -> p a n", a=E), other, own, ALU.is_gt)
                    last = v.tensor_tensor(equal[:, u, :].rearrange("p (a n) -> p a n", a=E), other, own, ALU.is_equal)
                link(last)
                link(v.tensor_tensor(equal[:, :, :], equal[:, :, :],
                                     lower[:, :].unsqueeze(1).to_broadcast([P, 4, E * E]), ALU.mult))
                link(v.tensor_tensor(above[:, :, :], above[:, :, :], equal[:, :, :], ALU.add))
                link(v.tensor_reduce(rank[:, :, :].rearrange("p a n -> p (a n)").unsqueeze(2),
                                     above[:, :, :].rearrange("p a (e n) -> p (a e) n", e=E), AX.X, ALU.add))

            def gate_weights(m):
                dve.wait_ge(exps_made, m + 1)
                link = gate_chain(m, 7)
                link(v.scalar_tensor_tensor(gt[:, :, :], rank[:, :, :], 1.5, ex[:, :, :], ALU.is_lt, ALU.mult))
                link(v.tensor_reduce(es[:, :].unsqueeze(2), gt[:, :, :], AX.X, ALU.add))
                link(v.reciprocal(er[:, :], es[:, :]))
                link(v.tensor_tensor(gt[:, :, :], gt[:, :, :], er[:, :].unsqueeze(2).to_broadcast([P, 4, E]), ALU.mult))
                link(v.tensor_copy(g24[:, :, 0:E], gt[:, :, :]))
                link(v.tensor_tensor(gr[:, :, :], gt[:, :, :], g24[:, :, 0:E], ALU.subtract))
                link(v.tensor_copy(g24[:, :, E:2 * E], gr[:, :, :]))
                v.tensor_tensor(g24[:, :, 2 * E:3 * E], gr[:, :, :], g24[:, :, E:2 * E],
                                ALU.subtract).then_inc(gate_step, 1)
                assert link.k + 1 == GATE_STEPS, link.k

            def gate_input(m, e):
                dve.wait_ge(gate_spread, E * m + e + 1)
                if e >= 2:
                    dve.wait_ge(expert_done, E * m + e - 1)
                v.tensor_tensor(zg[:, e % 2, :], ps0[:, :], y[:, :], ALU.mult).then_inc(gated, 1)

            def result(m, par):
                dve.wait_ge(expert_done, E * m + E)
                if not (isinstance(m, int) and m == 0):
                    dve.wait_ge(stored, 16 * m)
                v.tensor_tensor(ob[:, par, :], ps1[:, :], t1[:, :], ALU.add).then_inc(result_ready, 1)

            def chunk(b, c, n, par, ahead, first_half, second_half):
                for j in range(4):
                    shift(n, j)
                    if j == 2 and not (isinstance(c, int) and c == 0):
                        residual(c - 1, n - 1, 1 - par)
                for j in range(NP):
                    if ahead:
                        take_max(n + 1, j)
                    if j + 4 < NP:
                        shift(n, j + 4)
                    if first_half:
                        if j == 2:
                            ln_rsqrt(0, n - 1)
                        if j == 3:
                            ln_scale(0, n - 1)
                        if j == 4:
                            l1_keys_values(n - 1)
                        if j == 5:
                            add_windows(n - 1, tile_in_image(c, 1))
                    if second_half:
                        if j == 6:
                            l1_residual(n - 2, par)
                        if j == 8:
                            ln_rsqrt(1, n - 2)
                        if j == 9:
                            ln_scale(1, n - 2)
                        if j == 10:
                            gate_logits(n - 2)
                        if j == 11:
                            gate_weights(n - 2)
                        if j >= 13:
                            for e in ((0, 1), (2, 3, 4), (5, 6, 7))[j - 13]:
                                gate_input(n - 2, e)
                if second_half:
                    result(n - 2, par)
                if ahead:
                    fold_max(n + 1)
                invert_sums(n)
                if ahead:
                    query_maxima(n + 1)
                norm_heads(n)
                if not ahead:
                    residual(c, n, par)

            def finish():
                last = B * NCH
                ln_rsqrt(0, last - 1)
                ln_scale(0, last - 1)
                l1_keys_values(last - 1)
                add_windows(last - 1, NCH - 1)
                for m in (last - 2, last - 1):
                    l1_residual(m, m % 2)
                    ln_rsqrt(1, m)
                    ln_scale(1, m)
                    gate_logits(m)
                    gate_weights(m)
                    for e in range(E):
                        gate_input(m, e)
                    result(m, m % 2)

            walk(dve, prepare, first_scores, chunk, finish)

        @block.tensor
        def _(pe):
            mm = nc.tensor.matmul
            pe.wait_ge(consts_loaded, CONSTS)
            pe.wait_ge(consts_made, 3)

            def prepare(b, n0):
                pe.wait_ge(prep_step, PREP_STEPS * b + 4)
                mm(ps0[:, 0:2], group[:, :], chst[:, :], start=True, stop=True).then_inc(group_summed, 1)
                pe.wait_ge(prep_step, PREP_STEPS * b + H_STEP)
                for t in range(NCH):
                    i = NCH * b + t
                    tile = slice(t * T, (t + 1) * T)
                    if t >= 2:
                        pe.wait_ge(q_stored, i - 1)
                        pe.wait_ge(kv_held, 2 * i - 2)
                    mm(psS[:, t % 2, 0:T], wq_s[:, :], h[:, tile], start=True, stop=True).then_inc(q_made, 1)
                    mm(psS[:, t % 2, T:2 * T], wk_s[:, :], h[:, tile], start=True, stop=True)
                    for u in range(4):
                        last = mm((ps0, ps1)[t % 2][:, u * P:(u + 1) * P], h[:, t * T + u * P:t * T + (u + 1) * P],
                                  wv_s[:, :], start=True, stop=True)
                    last.then_inc(kv_made, 1)
                pe.wait_ge(absmax_taken, b + 1)
                mm(ps0[0:2, 0:P], am2[:, :], ident[:, :], start=True, stop=True).then_inc(absmax_turned, 1)
                pe.wait_ge(prep_step, PREP_STEPS * b + PREP_STEPS - 3)
                mm(ps0[:, 0:2], ones[0:2, :], amd[:, :], start=True, stop=True).then_inc(absmax_shared, 1)

            def scores(n, c, j, waits):
                if waits:
                    pe.wait_ge(max_taken, NP * n + j - 1)
                qs = bass.ds(c * T, T)
                for u in range(2):
                    key = slice((2 * j + u) * P, (2 * j + u + 1) * P)
                    dst = psS[:, j % 2, u * T:(u + 1) * T]
                    mm(dst, kh[:, key], qh[:, qs], start=True, stop=False)
                    mm(dst, kh[:, key], ql[:, qs], start=False, stop=False)
                    last = mm(dst, kl[:, key], qh[:, qs], start=False, stop=True)
                last.then_inc(scores_ready, 1)

            def values(n, j):
                pe.wait_ge(probs_ready, NP * n + j + 1)
                if j == 0 and not (isinstance(n, int) and n == 0):
                    pe.wait_ge(heads_copied, n)
                for u in range(2):
                    last = mm(psO[:, :], vs[:, 2 * j + u, :], st[:, j, u * T:(u + 1) * T],
                              start=(j == 0 and u == 0), stop=(j == NP - 1 and u == 1))
                last.then_inc(pv_done, 1)

            def turn_max(n):
                pe.wait_ge(max_folded, n + 1)
                for u in range(4):
                    last = nc.tensor.transpose(ps1[:, u * P:(u + 1) * P], mx[:, u * P:(u + 1) * P], ident[:, :])
                last.then_inc(max_turned, 1)

            def spread_max(n):
                pe.wait_ge(max_diag, n + 1)
                mm(psM[:, :], ones[:, :], dgm[:, :, :].rearrange("p a n -> p (a n)"), start=True,
                   stop=True).then_inc(max_spread, 1)

            def sum_rows(n):
                pe.wait_ge(rows_added, (NP - 1) * n + NP - 1)
                for u in range(4):
                    for half in range(2):
                        at = half * T + u * P
                        last = mm(ps0[:, u:u + 1], rs[:, at:at + P], ones[:, 0:1], start=(half == 0), stop=(half == 1))
                last.then_inc(sums_ready, 1)

            def spread_sums(n):
                pe.wait_ge(sums_diag, n + 1)
                mm(ps0[:, :], ones[:, :], dgl[:, :, :].rearrange("p a n -> p (a n)"), start=True,
                   stop=True).then_inc(sums_spread, 1)

            def mix_heads(n):
                pe.wait_ge(heads_normed, n + 1)
                mm(ps1[:, :], wo_s[:, :], osb[:, :], start=True, stop=True).then_inc(heads_mixed, 1)

            def first_scores(b, n0):
                pe.wait_ge(low_parts, 2 * b + 2)
                for j in range(NP):
                    scores(n0, 0, j, j >= 2)
                turn_max(n0)
                for j in range(2):
                    scores(n0 + 1, 1, j, True)
                spread_max(n0)

            def ln_center(k, m, src, ready):
                pe.wait_ge(ready, m + 1)
                mm(ps0[:, :], center[:, :], src, start=True, stop=True).then_inc(centered[k], 1)

            def ln_variance(k, m):
                pe.wait_ge(squared[k], m + 1)
                for u in range(4):
                    last = mm(ps0[:, u:u + 1], sq[:, u * P:(u + 1) * P], meancol[:, :], start=True, stop=True)
                last.then_inc(var_ready[k], 1)

            def ln_spread_rsqrt(k, m):
                pe.wait_ge(ln_diag[k], m + 1)
                mm(ps0[:, :], ones[:, :], dgn[:, :, :].rearrange("p a n -> p (a n)"), start=True,
                   stop=True).then_inc(ln_spread[k], 1)

            def l1_projections(m):
                pe.wait_ge(normed[0], m + 1)
                mm(ps1[:, :], wq1_s[:, :], y[:, :], start=True, stop=True).then_inc(l1_q_made, 1)
                for i, bank in enumerate((ps0, ps1)):
                    if i:
                        pe.wait_ge(l1_q_stored, m + 1)
                    for u in range(2):
                        last = mm(bank[:, 2 * u * P:2 * (u + 1) * P], y[:, (2 * i + u) * P:(2 * i + u + 1) * P],
                                  wkv1_s[:, :], start=True, stop=True)
                    last.then_inc(l1_kv_made, 1)

            def l1_blocks(m):
                pe.wait_ge(edges_masked, m + 1)
                for i, bank in enumerate((ps0, ps1)):
                    for u in range(2):
                        last = mm(bank[:, 0:3 * P], k3[:, 2 * i + u, :],
                                  v3[:, 2 * i + u, :, :].rearrange("p a n -> p (a n)"), start=(u == 0), stop=(u == 1))
                    last.then_inc(block_summed, 1)

            def l1_attend(m, par):
                pe.wait_ge(window_scaled, m + 1)
                pe.wait_ge(l1_q_stored, m + 1)
                for i in range(2):
                    last = mm(ps0[:, 2 * i * P:2 * (i + 1) * P], mcur[:, i, :], q1[:, par, 2 * i * P:2 * (i + 1) * P],
                              start=True, stop=True)
                last.then_inc(attended, 1)

            def router(m):
                pe.wait_ge(normed[1], m + 1)
                for u in range(4):
                    last = mm(ps0[:, u * E:(u + 1) * E], y[:, u * P:(u + 1) * P], rw_s[:, :], start=True, stop=True)
                last.then_inc(logits_made, 1)

            def turn_gates(m):
                pe.wait_ge(gate_step, GATE_STEPS * m + GATE_STEPS)
                dst = ps0[0:GPARTS * E, 0:T // 2].bitcast(bf16)
                for u in range(4):
                    last = nc.tensor.transpose(dst[:, u * P:(u + 1) * P], g24[:, u, :], identb[:, :])
                last.then_inc(gates_turned, 1)

            def expert_bias(m):
                pe.wait_ge(gates_stored, 2 * m + 2)
                mm(ps1[:, :], eb_s[:, :], gTf, start=True, stop=False)

            def spread_gate(m, e):
                if e:
                    pe.wait_ge(gated, E * m + e)
                mm(ps0[:, :], sel[:, e, :], gT[:, :], start=True, stop=True).then_inc(gate_spread, 1)

            def expert(m, e):
                pe.wait_ge(gated, E * m + e + 1)
                mm(ps1[:, :], ew_s[:, e, :], zg[:, e % 2, :], start=False, stop=(e == E - 1)).then_inc(expert_done, 1)

            def experts(m, es):
                for e in es:
                    if e == 0:
                        expert_bias(m)
                        spread_gate(m, 0)
                    elif e == E:
                        expert(m, E - 1)
                        continue
                    if e:
                        spread_gate(m, e)
                        expert(m, e - 1)

            def chunk(b, c, n, par, ahead, first_half, second_half):
                for j in range(NP):
                    values(n, j)
                    if ahead and j >= 2:
                        scores(n + 1, c + 1, j, True)
                    if first_half:
                        if j == 1:
                            ln_center(0, n - 1, tt[:, 1 - par, :], layer0_out)
                        if j == 2:
                            ln_variance(0, n - 1)
                        if j == 3:
                            ln_spread_rsqrt(0, n - 1)
                        if j == 4:
                            l1_projections(n - 1)
                        if j == 5:
                            l1_blocks(n - 1)
                    if second_half:
                        if j == 6:
                            l1_attend(n - 2, par)
                        if j == 7:
                            ln_center(1, n - 2, t1[:, :], t1_ready)
                        if j == 8:
                            ln_variance(1, n - 2)
                        if j == 9:
                            ln_spread_rsqrt(1, n - 2)
                        if j == 10:
                            router(n - 2)
                        if j == 12:
                            turn_gates(n - 2)
                        if j >= 13:
                            experts(n - 2, ((0, 1), (2, 3, 4), (5, 6, 7, 8))[j - 13])
                if second_half:
                    pe.wait_ge(result_ready, n - 1)
                sum_rows(n)
                if ahead:
                    turn_max(n + 1)
                if ahead == 2:
                    for j in range(2):
                        scores(n + 2, c + 2, j, True)
                if ahead:
                    spread_max(n + 1)
                spread_sums(n)
                mix_heads(n)

            def finish():
                last = B * NCH
                ln_center(0, last - 1, tt[:, 1, :], layer0_out)
                ln_variance(0, last - 1)
                ln_spread_rsqrt(0, last - 1)
                l1_projections(last - 1)
                l1_blocks(last - 1)
                for m in (last - 2, last - 1):
                    l1_attend(m, m % 2)
                    ln_center(1, m, t1[:, :], t1_ready)
                    ln_variance(1, m)
                    ln_spread_rsqrt(1, m)
                    router(m)
                    turn_gates(m)
                    if m == last - 1:
                        pe.wait_ge(result_ready, m)
                    experts(m, range(E + 1))

            walk(pe, prepare, first_scores, chunk, finish)


def kernel(**inputs):
    import numpy as np
    import concourse.bacc as bacc
    from concourse.bass_utils import run_bass_kernel_spmd

    def arr(name):
        return np.ascontiguousarray(inputs[name])

    def col(name):
        return arr(name).reshape(-1, 1)

    def rows(a, n=128):
        return np.ascontiguousarray(np.broadcast_to(a.reshape(1, -1), (n, a.size)))

    x = arr("x")
    b, c, hh, ww = x.shape
    e = inputs["L1_ffn_router_w"].shape[1]
    f = np.float32
    group = np.zeros((c, c), f)
    for g in range(0, c, 4):
        group[g:g + 4, g:g + 4] = 0.25
    center = np.full((c, c), -1.0 / c, f)
    center[np.arange(c), np.arange(c)] = 1.0 - 1.0 / c
    sel = np.zeros((3 * e, e * 128), f)
    lower = np.zeros((e, e), f)
    for i in range(e):
        for part in range(3):
            sel[part * e + i, i * 128:(i + 1) * 128] = 1.0
        lower[i, :i] = 1.0
    notlast = np.ones((128, 1), f)
    notlast[127] = 0.0
    w1 = "L1_attn_W"
    arrays = {
        "x_in": x.reshape(b, c, hh * ww),
        "norm_w": col("L0_conv_norm_w"), "norm_b": col("L0_conv_norm_b"),
        "wq": arr("L0_conv_Wq"), "bq": col("L0_conv_bq"),
        "wk": arr("L0_conv_Wk"), "bk": col("L0_conv_bk"),
        "wv": arr("L0_conv_Wv"), "bv_rows": rows(arr("L0_conv_bv")),
        "wo": arr("L0_conv_Wo"), "bo": col("L0_conv_bo"),
        "l1_wqT": np.ascontiguousarray(arr(w1 + "q").T), "l1_bq": col("L1_attn_bq"),
        "l1_wkvT": np.ascontiguousarray(np.concatenate([arr(w1 + "k").T, arr(w1 + "v").T], axis=1)),
        "l1_bkv_rows": rows(np.concatenate([arr("L1_attn_bk"), arr("L1_attn_bv")])),
        "router_w": arr("L1_ffn_router_w"), "router_b_rows": rows(arr("L1_ffn_router_b")),
        "expert_w": arr("L1_ffn_expert_w"),
        "expert_b3": np.ascontiguousarray(np.tile(arr("L1_ffn_expert_b"), (3, 1))),
        "c_ident": np.eye(128, dtype=f), "c_center": center,
        "c_mean": np.full((128, 1), 1.0 / c, f), "c_group": group,
        "c_sel": sel, "c_lower": rows(lower), "c_notlast": notlast,
    }
    nc = bacc.Bacc("TRN2", target_bir_lowering=False, num_devices=1)
    args = [nc.dram_tensor(n, a.shape, mybir.dt.float32, kind="ExternalInput").ap() for n, a in arrays.items()]
    args.append(nc.dram_tensor("out", (b, c, hh * ww), mybir.dt.float32, kind="ExternalOutput").ap())
    conv_attn_hybrid_kernel(nc, *args)
    r = run_bass_kernel_spmd(nc, [arrays], core_ids=[0])
    return r.results[0]["out"].reshape(b, c, hh, ww)
```

```python
import concourse.bass as bass
from concourse import mybir
from contextlib import ExitStack



def conv_attn_hybrid_kernel(nc, x, norm_w, norm_b, wq, bq, wk, bk, wv, bv_rows, wo, bo,
                            l1_wqT, l1_bq, l1_wkvT, l1_bkv_rows, router_w, router_b_rows,
                            expert_w, expert_b3, c_ident, c_center, c_mean, c_group, c_sel, c_lower,
                c_edges, out):
    fp32, bf16, fp16, i32 = mybir.dt.float32, mybir.dt.bfloat16, mybir.dt.float16, mybir.dt.int32
    ALU = mybir.AluOpType
    ACT = mybir.ActivationFunctionType
    AX = mybir.AxisListType

    B, C, N = x.shape
    P = 128
    T = 512
    NCH = N // T
    KT = N // P
    NP = KT // 2
    E = router_w.shape[1]
    GPARTS = 3
    NB = N // 256
    GN_EPS = LN_EPS = 1e-5
    TOP = 16384.0
    RSQRT_SEED = float(0x5F3759DF)
    RSQRT_STEPS = 12
    LAG = 3
    PREP_STEPS = 27
    H_STEP = 21
    GATE_STEPS = 15

    ctx = ExitStack()
    with ctx:
        def sb(name, shape, dt=fp32):
            return ctx.enter_context(nc.sbuf_tensor(name, shape, dt))

        def pb(name, shape):
            return ctx.enter_context(nc.psum_tensor(name, shape, fp32))

        def sem(name):
            return ctx.enter_context(nc.semaphore(name))

        ident = sb("ident", [P, P])
        identb = sb("identb", [P, P], bf16)
        center = sb("center", [P, P])
        meancol = sb("meancol", [P, 1])
        group = sb("group", [P, P])
        ones = sb("ones", [P, P])
        sel = sb("sel", [E * GPARTS, E, P], bf16)
        lower = sb("lower", [P, E * E])
        edges = sb("edges", [P, 2, 4])
        wq_s, wk_s, wv_s, wo_s = (sb(n, [P, P]) for n in ("wq_s", "wk_s", "wv_s", "wo_s"))
        wq1_s = sb("wq1_s", [P, P])
        wkv1_s = sb("wkv1_s", [P, 2 * P])
        cols = sb("cols", [P, 6])
        gw_c, gb_c, bq_c, bk_c, bo_c, bq1_c = (cols[:, i:i + 1] for i in range(6))
        bv_s = sb("bv_s", [P, P])
        bkv1_s = sb("bkv1_s", [P, 2 * P])
        rw_s = sb("rw_s", [P, E])
        rb_s = sb("rb_s", [P, E])
        ew_s = sb("ew_s", [P, E, P])
        eb_s = sb("eb_s", [E * GPARTS, P])

        xs = sb("xs", [P, N])
        qh, ql, kh, kl = (sb(n, [P, N], fp16) for n in ("qh", "ql", "kh", "kl"))
        vs = sb("vs", [P, KT, P])
        st = sb("st", [P, NP, 2 * T])
        self32 = st[0:E * GPARTS, NP - 1, 0:E * P]
        temps = st[:, :, :].rearrange("p a n -> p (a n)")
        h = temps[:, 0:N]
        qf, kf = temps[:, N:2 * N], temps[:, 2 * N:3 * N]
        qkf = temps[:, N:3 * N].rearrange("p (a n) -> p a n", a=2)
        bstats = sb("bstats", [P, NCH, 6])
        chst = sb("chst", [P, 2])
        gst = sb("gst", [P, 2])
        gsm = sb("gsm", [P, 8])
        amx = sb("amx", [P, 2, NCH])
        am2 = sb("am2", [P, 2])
        amr = sb("amr", [2, 1])
        amd = sb("amd", [2, 2])
        ag = sb("ag", [P, 2])
        iv = sb("iv", [P, 2])
        sc = sb("sc", [P, 1])

        acc = sb("acc", [P, 2, T])
        mx = acc[:, 0, :]
        mq = sb("mq", [P, 4])
        dgm = sb("dgm", [P, 4, P])
        rs = sb("rs", [P, 2 * T])
        rl = sb("rl", [P, 4])
        dgl = sb("dgl", [P, 4, P])
        osb = sb("osb", [P, T])

        tt = sb("tt", [P, 2, T])
        xc = sb("xc", [P, T])
        sq = sb("sq", [P, T])
        rsm = [sb(f"rsm{k}", [P, 4, 4]) for k in range(2)]
        dgn = sb("dgn", [P, 4, P])
        y = sb("y", [P, T])
        z = sb("z", [P, T])
        q1 = sb("q1", [P, 2, T])
        k3 = sb("k3", [P, 4, P])
        v3 = sb("v3", [P, 4, 3, P])
        mst = sb("mst", [P, (NB + 2) * P])
        mcur = sb("mcur", [P, 2, P])
        t1 = sb("t1", [P, T])
        lg, ex, em, gt, gr = (sb(n, [P, 4, E]) for n in ("lg", "ex", "em", "gt", "gr"))
        lm, es, er = (sb(n, [P, 4]) for n in ("lm", "es", "er"))
        above, equal = (sb(n, [P, 4, E * E]) for n in ("above", "equal"))
        rank = sb("rank", [P, 4, E])
        g24 = sb("g24", [P, 4, GPARTS * E], bf16)
        gT = sb("gT", [GPARTS * E, T], bf16)
        gTf = sb("gTf", [GPARTS * E, T])[:, :]
        zg = sb("zg", [P, 2, T])
        ob = sb("ob", [P, T])

        SB = 3
        psS = pb("psS", [P, SB, T])
        psM = pb("psM", [P, T])
        psO = pb("psO", [P, T])
        ps0 = pb("ps0", [P, T])
        ps1 = pb("ps1", [P, T])
        ps2 = pb("ps2", [P, T])

        consts_loaded, consts_made, x_loaded = sem("consts_loaded"), sem("consts_made"), sem("x_loaded")
        prep_step, group_summed, h_read = sem("prep_step"), sem("group_summed"), sem("h_read")
        q_made, kv_made = sem("q_made"), sem("kv_made")
        q_stored, kv_held, absmax_taken, absmax_turned = (
            sem(n) for n in ("q_stored", "kv_held", "absmax_taken", "absmax_turned"))
        absmax_shared, high_parts, low_parts = sem("absmax_shared"), sem("high_parts"), sem("low_parts")
        scores_ready, scores_copied, max_taken, shifted = (
            sem(n) for n in ("scores_ready", "scores_copied", "max_taken", "shifted"))
        probs_ready, pv_done, rows_added = sem("probs_ready"), sem("pv_done"), sem("rows_added")
        max_folded, max_turned, query_max, max_diag, max_spread = (
            sem(n) for n in ("max_folded", "max_turned", "query_max", "max_diag", "max_spread"))
        sums_ready, sums_inverted, sums_diag, sums_spread = (
            sem(n) for n in ("sums_ready", "sums_inverted", "sums_diag", "sums_spread"))
        heads_copied, heads_normed, heads_mixed, layer0_out = (
            sem(n) for n in ("heads_copied", "heads_normed", "heads_mixed", "layer0_out"))
        centered, center_copied, squared, var_ready, rsqrt_step, ln_diag, ln_spread, normed = (
            [sem(f"{n}{k}") for k in range(2)] for n in
            ("centered", "center_copied", "squared", "var_ready", "rsqrt_step", "ln_diag", "ln_spread", "normed"))
        l1_q_made, l1_q_stored, l1_kv_made, l1_kv_stored, edges_masked, block_summed, window_added = (
            sem(n) for n in ("l1_q_made", "l1_q_stored", "l1_kv_made", "l1_kv_stored", "edges_masked",
                             "block_summed", "window_added"))
        window_scaled, attended, t1_ready, logits_made, gate_step, exps_made = (
            sem(n) for n in ("window_scaled", "attended", "t1_ready", "logits_made", "gate_step", "exps_made"))
        gates_turned, gates_stored, gate_spread, gated, expert_done, result_ready, stored = (
            sem(n) for n in ("gates_turned", "gates_stored", "gate_spread", "gated", "expert_done",
                             "result_ready", "stored"))

        block = ctx.enter_context(nc.Block())

        n_const = [0]

        def walk(eng, prepare, first_scores, chunk, side):
            def image(b, n0, first):
                prepare(b, n0)
                first_scores(b, n0)
                if first:
                    for c in range(NCH - 2):
                        chunk(b, c, c, c % 2, 2)
                else:
                    chunk(b, 0, n0, 0, 2)
                    chunk(b, 1, n0 + 1, 1, 2)
                    with eng.Fori(1, NCH // 2 - 1) as twos:
                        c = twos * 2
                        chunk(b, c, n0 + c, 0, 2)
                        chunk(b, c + 1, n0 + c + 1, 1, 2)
                chunk(b, NCH - 2, n0 + NCH - 2, 0, 1)
                chunk(b, NCH - 1, n0 + NCH - 1, 1, 0)
            image(0, 0, True)
            with eng.Fori(1, B) as b:
                image(b, b * NCH, False)
            for n in range(B * NCH, B * NCH + LAG):
                for j in range(NP):
                    side(n, n % NCH, n % 2, j)

        def has(n, lag):
            return not isinstance(n, int) or lag <= n < B * NCH + lag

        def tile_in_image(c, back):
            return (c - back) % NCH if isinstance(c, int) else c - back

        @block.sync
        def _(sp):
            def const(dst, src):
                sp.dma_start(dst, src).then_inc(consts_loaded, 16)
                n_const[0] += 16
            for i, v in enumerate((norm_w, norm_b, bq, bk, bo, l1_bq)):
                const(cols[:, i:i + 1], v)
            for dst, src in ((group, c_group), (wq_s, wq), (wk_s, wk), (wv_s, wv), (bv_s, bv_rows)):
                const(dst[:, :], src)

            def load_x(b):
                sp.dma_start(xs[:, :], x[bass.ds(b, 1), :, :].rearrange("a c n -> (a c) n")).then_inc(x_loaded, 16)

            def store(m, b, j):
                sp.wait_ge(result_ready, m + 1)
                sp.dma_start(out[bass.ds(b, 1), :, j * T:(j + 1) * T].rearrange("a c n -> (a c) n"),
                             ob[:, :]).then_inc(stored, 16)

            load_x(0)
            for dst, src in ((ident, c_ident), (center, c_center), (wo_s, wo), (lower, c_lower), (wq1_s, l1_wqT),
                             (wkv1_s, l1_wkvT), (bkv1_s, l1_bkv_rows), (rw_s, router_w), (rb_s, router_b_rows),
                             (eb_s, expert_b3), (meancol, c_mean)):
                const(dst[:, :], src)
            const(self32, c_sel)
            const(edges[:, :, :].rearrange("p a n -> p (a n)"), c_edges)
            const(ew_s[:, :, :], expert_w.rearrange("e d c -> d e c"))
            for m in range(NCH - LAG):
                store(m, 0, m)
            with sp.Fori(1, B) as b:
                sp.wait_ge(layer0_out, b * NCH)
                load_x(b)
                for m in range(NCH - LAG, NCH):
                    store((b - 1) * NCH + m, b - 1, m)
                for m in range(NCH - LAG):
                    store(b * NCH + m, b, m)
            for m in range(NCH - LAG, NCH):
                store((B - 1) * NCH + m, B - 1, m)
            sp.wait_ge(stored, 16 * B * NCH)

        CONSTS = n_const[0]

        @block.gpsimd
        def _(pool):
            nc.gpsimd.memset(ones[:, :], 1.0).then_inc(consts_made, 1)

            def ln_diagonal(k, m):
                pool.wait_ge(rsqrt_step[k], RSQRT_STEPS * m + RSQRT_STEPS)
                if not (isinstance(m, int) and m == 0):
                    pool.wait_ge(ln_spread[k], m)
                nc.gpsimd.tensor_tensor(dgn[:, :, :], ident[:, :].unsqueeze(1).to_broadcast([P, 4, P]),
                                        rsm[k][:, 3, :].unsqueeze(2).to_broadcast([P, 4, P]),
                                        ALU.mult).then_inc(ln_diag[k], 1)

            def add_rows(n, j):
                pool.wait_ge(probs_ready, NP * n + j + 1)
                if j == 1:
                    if not (isinstance(n, int) and n == 0):
                        pool.wait_ge(sums_ready, n)
                    a = st[:, 0, :]
                else:
                    pool.wait_ge(rows_added, NP * n + j - 1)
                    a = rs[:, :]
                nc.gpsimd.tensor_tensor(rs[:, :], a, st[:, j, :], ALU.add).then_inc(rows_added, 1)

            def fold_rows(n):
                pool.wait_ge(rows_added, NP * n + NP - 1)
                nc.gpsimd.tensor_tensor(rs[:, 0:T], rs[:, 0:T], rs[:, T:2 * T], ALU.add).then_inc(rows_added, 1)

            def mask_edges(m):
                pool.wait_ge(l1_kv_stored, 2 * m + 2)
                for s in (0, 1):
                    last = nc.gpsimd.tensor_tensor(v3[:, :, 2 * s, :], v3[:, :, 1, :],
                                                   edges[:, s, :].unsqueeze(2).to_broadcast([P, 4, P]), ALU.mult)
                last.then_inc(edges_masked, 1)

            def side(n, c, par, j):
                if j == 3 and has(n, 1):
                    ln_diagonal(0, n - 1)
                if j == 8 and has(n, 1):
                    mask_edges(n - 1)
                if j == 15 and has(n, 2):
                    ln_diagonal(1, n - 2)

            def chunk(b, c, n, par, ahead):
                for j in range(NP):
                    if j:
                        add_rows(n, j)
                    side(n, c, par, j)
                fold_rows(n)

            pool.wait_ge(consts_loaded, CONSTS)
            walk(pool, lambda b, n0: None, lambda b, n0: None, chunk, side)

        @block.scalar
        def _(act):
            act.wait_ge(consts_loaded, CONSTS)
            nc.scalar.activation(sel[:, :, :].rearrange("p a n -> p (a n)"), self32, ACT.Copy).then_inc(consts_made, 1)
            nc.scalar.activation(identb[:, :], ident[:, :], ACT.Copy).then_inc(consts_made, 1)

            def prepare(b, n0):
                for t in range(NCH):
                    act.wait_ge(q_made, NCH * b + t + 1)
                    nc.scalar.activation(qf[:, t * T:(t + 1) * T], psS[:, t % 2, :], ACT.Identity,
                                         bias=bq_c).then_inc(q_stored, 1)
                act.wait_ge(prep_step, PREP_STEPS * b + PREP_STEPS)
                for dst, src, s in ((kh, kf, 1), (qh, qf, 0)):
                    nc.scalar.activation(dst[:, :], src, ACT.Copy, scale=iv[:, s:s + 1]).then_inc(high_parts, 1)

            def copy_scores(n, k, first):
                act.wait_ge(scores_ready, KT * n + k + 1)
                if not first:
                    act.wait_ge(pv_done, NP * (n - 1) + k // 2 + 1)
                    act.wait_ge(rows_added, NP * (n - 1) + max(k // 2, 1))
                nc.scalar.activation(st[:, k // 2, (k % 2) * T:(k % 2 + 1) * T], psS[:, k % SB, :],
                                     ACT.Copy).then_inc(scores_copied, 1)

            def exponentiate(n, j):
                act.wait_ge(shifted, NP * n + j + 1)
                nc.scalar.activation(st[:, j, :], st[:, j, :], ACT.Exp, scale=sc[:, :]).then_inc(probs_ready, 1)

            def first_scores(b, n0):
                act.wait_ge(low_parts, 2 * b + 2)
                for k in range(KT):
                    copy_scores(n0, k, True)

            def ln_center(k, m):
                act.wait_ge(centered[k], m + 1)
                nc.scalar.activation(xc[:, :], ps0[:, :], ACT.Copy).then_inc(center_copied[k], 1)
                act.wait_ge(center_copied[k], m + 1)
                nc.scalar.activation(sq[:, :], xc[:, :], ACT.Square).then_inc(squared[k], 1)

            def l1_query(m, par):
                act.wait_ge(l1_q_made, m + 1)
                nc.scalar.activation(q1[:, par, :], ps0[:, :], ACT.Identity, bias=bq1_c).then_inc(l1_q_stored, 1)

            def scale_window(m, j, tiles_added):
                act.wait_ge(window_added, 4 * tiles_added)
                nc.scalar.activation(mcur[:, :, :].rearrange("p a n -> p (a n)"),
                                     mst[:, bass.ds((2 * j + 1) * P, 2 * P)], ACT.Copy,
                                     scale=float(C) ** -0.5).then_inc(window_scaled, 1)

            def exp_logits(m):
                act.wait_ge(gate_step, GATE_STEPS * m + 3)
                nc.scalar.activation(ex[:, :, :], em[:, :, :], ACT.Exp).then_inc(exps_made, 1)

            def store_gates(m):
                act.wait_ge(gates_turned, m + 1)
                nc.scalar.activation(gT[:, :], ps2[0:GPARTS * E, 0:T // 2].bitcast(bf16), ACT.Copy).then_inc(gates_stored, 1)
                act.wait_ge(gates_stored, 2 * m + 1)
                nc.scalar.activation(gTf, gT[:, :], ACT.Copy).then_inc(gates_stored, 1)

            def copy_heads(n):
                act.wait_ge(pv_done, NP * n + NP)
                nc.scalar.activation(osb[:, :], psO[:, :], ACT.Copy).then_inc(heads_copied, 1)

            def side(n, c, par, j):
                if has(n, 1):
                    if j == 1:
                        ln_center(0, n - 1)
                    if j == 5:
                        l1_query(n - 1, 1 - par)
                if has(n, 2):
                    if j == 11:
                        scale_window(n - 2, tile_in_image(c, 2), min(n, B * NCH) if isinstance(n, int) else n)
                    if j == 13:
                        ln_center(1, n - 2)
                if has(n, 3):
                    if j == 1:
                        exp_logits(n - 3)
                    if j == 3:
                        store_gates(n - 3)

            def chunk(b, c, n, par, ahead):
                for j in range(3):
                    exponentiate(n, j)
                for j in range(NP):
                    if ahead:
                        copy_scores(n + 1, 2 * j, False)
                        copy_scores(n + 1, 2 * j + 1, False)
                    side(n, c, par, j)
                    if j + 3 < NP:
                        exponentiate(n, j + 3)
                copy_heads(n)

            walk(act, prepare, first_scores, chunk, side)

        @block.vector
        def _(dve):
            v = nc.vector
            dve.wait_ge(consts_loaded, CONSTS)

            def rsqrt(var, s, step, base, k0):
                def link(ins):
                    ins.then_inc(step, 1)
                    link.k += 1
                    dve.wait_ge(step, base + link.k)
                link.k = k0
                link(v.tensor_scalar(s[1].bitcast(i32), s[0].bitcast(i32), 1, None, ALU.logical_shift_right))
                link(v.tensor_scalar(s[3].bitcast(i32), s[1].bitcast(i32), -1.0, RSQRT_SEED, ALU.mult, ALU.add))
                for _ in range(3):
                    link(v.tensor_tensor(s[1], s[3], s[3], ALU.mult))
                    link(v.scalar_tensor_tensor(s[2], s[1], -0.5, s[0], ALU.mult, ALU.mult))
                    link(v.scalar_tensor_tensor(s[3], s[2], 1.5, s[3], ALU.add, ALU.mult))
                return link.k

            def prepare(b, n0):
                base = PREP_STEPS * b
                k = 0

                def link(ins):
                    nonlocal k
                    ins.then_inc(prep_step, 1)
                    k += 1
                    dve.wait_ge(prep_step, base + k)

                dve.wait_ge(x_loaded, 16 * b + 16)
                for t in range(NCH):
                    last = v.bn_stats(bstats[:, t, :], xs[:, t * T:(t + 1) * T])
                if not isinstance(b, int):
                    dve.wait_ge(window_scaled, n0 - 2)
                link(last)
                v.memset(mst[:, 0:2 * P], 0.0).then_inc(prep_step, 1)
                k += 1
                link(v.bn_aggr(chst[:, :], bstats[:, :, :].rearrange("p a n -> p (a n)")))
                link(v.scalar_tensor_tensor(chst[:, 1:2], chst[:, 0:1], chst[:, 0:1], chst[:, 1:2], ALU.mult, ALU.add))
                dve.wait_ge(group_summed, b + 1)
                link(v.tensor_copy(gst[:, :], ps0[:, 0:2]))
                s = [gsm[:, i:i + 1] for i in range(8)]
                link(v.scalar_tensor_tensor(s[4], gst[:, 0:1], gst[:, 0:1], gst[:, 1:2], ALU.mult, ALU.subtract))
                link(v.tensor_scalar(s[0], s[4], -1.0, GN_EPS, ALU.mult, ALU.add))
                k = rsqrt(None, s, prep_step, base, k)
                link(v.tensor_tensor(s[5], s[3], gw_c, ALU.mult))
                link(v.scalar_tensor_tensor(s[6], gst[:, 0:1], s[5], gb_c, ALU.mult, ALU.subtract))
                if not isinstance(b, int):
                    dve.wait_ge(pv_done, NP * n0)
                    dve.wait_ge(rows_added, NP * n0)
                link(v.tensor_scalar(h, xs[:, :], s[5], s[6], ALU.mult, ALU.subtract))
                for t in range(NCH):
                    i = NCH * b + t
                    tile = slice(t * T, (t + 1) * T)
                    dve.wait_ge(kv_made, i + 1)
                    v.tensor_scalar(kf[:, tile], (psS[:, 2, :], psM[:, :])[t % 2], bk_c, None, ALU.add).then_inc(kv_held, 1)
                    v.tensor_tensor(vs[:, 4 * t:4 * t + 4, :], (ps0, ps1)[t % 2][:, :].rearrange("p (a n) -> p a n", a=4),
                                    bv_s[:, :].unsqueeze(1).to_broadcast([P, 4, P]), ALU.add).then_inc(kv_held, 1)
                    dve.wait_ge(q_stored, i + 1)
                    dve.wait_ge(kv_held, 2 * i + 2)
                    last = v.tensor_reduce(amx[:, :, t:t + 1], qkf[:, :, tile], AX.X, ALU.max,
                                           apply_absolute_value=True)
                link(last)
                v.tensor_reduce(am2[:, :].unsqueeze(2), amx[:, :, :], AX.X, ALU.max).then_inc(absmax_taken, 1)
                dve.wait_ge(absmax_turned, b + 1)
                link(v.tensor_reduce(amr[:, :], ps0[0:2, 0:P], AX.X, ALU.max))
                v.tensor_scalar(amd[:, :], ident[0:2, 0:2], amr[:, :], None, ALU.mult).then_inc(prep_step, 1)
                k += 1
                dve.wait_ge(absmax_shared, b + 1)
                link(v.tensor_scalar(ag[:, :], ps0[:, 0:2], 1e-30, None, ALU.max))
                v.tensor_scalar(sc[:, :], ag[:, 0:1], ag[:, 1:2], float(C) ** -0.5 / TOP ** 2, ALU.mult, ALU.mult)
                link(v.reciprocal(iv[:, :], ag[:, :]))
                v.tensor_scalar(iv[:, :], iv[:, :], TOP, None, ALU.mult).then_inc(prep_step, 1)
                k += 1
                assert k == PREP_STEPS, k
                dve.wait_ge(prep_step, base + PREP_STEPS)
                for i, (lo, hi, src, s) in enumerate(((kl, kh, kf, 1), (ql, qh, qf, 0))):
                    dve.wait_ge(high_parts, 2 * b + i + 1)
                    v.scalar_tensor_tensor(lo[:, :], src, iv[:, s:s + 1], hi[:, :], ALU.mult,
                                           ALU.subtract).then_inc(low_parts, 1)

            def take_max(n, k):
                dve.wait_ge(scores_copied, KT * n + k + 1)
                half = acc[:, k % 2, :]
                if k < 2:
                    v.tensor_copy(half, psS[:, k % SB, :]).then_inc(max_taken, 1)
                else:
                    dve.wait_ge(max_taken, KT * n + k - 1)
                    v.tensor_tensor(half, psS[:, k % SB, :], half, ALU.max).then_inc(max_taken, 1)

            def fold_max(n):
                dve.wait_ge(max_taken, KT * n + KT)
                v.tensor_tensor(mx, acc[:, 0, :], acc[:, 1, :], ALU.max).then_inc(max_folded, 1)

            def diagonal(dst, col):
                return v.tensor_tensor(dst[:, :, :], ident[:, :].unsqueeze(1).to_broadcast([P, 4, P]),
                                       col.unsqueeze(2).to_broadcast([P, 4, P]), ALU.mult)

            def query_maxima(n):
                dve.wait_ge(max_turned, n + 1)
                v.tensor_reduce(mq[:, :].unsqueeze(2), ps1[:, :].rearrange("p (a n) -> p a n", a=4), AX.X,
                                ALU.max).then_inc(query_max, 1)
                dve.wait_ge(query_max, n + 1)
                if not (isinstance(n, int) and n == 0):
                    dve.wait_ge(max_spread, n)
                diagonal(dgm, mq[:, :]).then_inc(max_diag, 1)

            def invert_sums(n):
                dve.wait_ge(sums_ready, n + 1)
                v.reciprocal(rl[:, :], ps2[:, 0:4]).then_inc(sums_inverted, 1)
                dve.wait_ge(sums_inverted, n + 1)
                if not (isinstance(n, int) and n == 0):
                    dve.wait_ge(sums_spread, n)
                diagonal(dgl, rl[:, :]).then_inc(sums_diag, 1)

            def norm_heads(n):
                dve.wait_ge(sums_spread, n + 1)
                dve.wait_ge(heads_copied, n + 1)
                v.tensor_tensor(osb[:, :], ps2[:, :], osb[:, :], ALU.mult).then_inc(heads_normed, 1)

            def residual(c, n, par):
                dve.wait_ge(heads_mixed, n + 1)
                v.scalar_tensor_tensor(tt[:, par, :], ps1[:, :], bo_c, xs[:, bass.ds(c * T, T)], ALU.add,
                                       ALU.add).then_inc(layer0_out, 1)

            def shift(n, j):
                if j == 0:
                    dve.wait_ge(max_spread, n + 1)
                pair = st[:, j, :].rearrange("p (a n) -> p a n", a=2)
                v.tensor_tensor(pair, pair, psM[:, :].unsqueeze(1).to_broadcast([P, 2, T]),
                                ALU.subtract).then_inc(shifted, 1)

            def first_scores(b, n0):
                for k in range(KT):
                    take_max(n0, k)
                fold_max(n0)
                query_maxima(n0)

            def ln_rsqrt(k, m):
                dve.wait_ge(var_ready[k], m + 1)
                s = [rsm[k][:, i, :] for i in range(4)]
                base = RSQRT_STEPS * m
                v.tensor_scalar(s[0], ps0[:, 0:4], LN_EPS, None, ALU.add).then_inc(rsqrt_step[k], 1)
                dve.wait_ge(rsqrt_step[k], base + 1)
                assert rsqrt(None, s, rsqrt_step[k], base, 1) == RSQRT_STEPS

            def ln_scale(k, m, dst):
                dve.wait_ge(ln_spread[k], m + 1)
                v.tensor_tensor(dst[:, :], ps0[:, :], xc[:, :], ALU.mult).then_inc(normed[k], 1)

            def l1_keys_values(m, i):
                dve.wait_ge(l1_kv_made, 2 * m + i + 1)
                kv = ps0[:, :].rearrange("p (a n) -> p a n", a=2)
                v.tensor_tensor(k3[:, 2 * i:2 * i + 2, :], kv[:, :, 0:P],
                                bkv1_s[:, 0:P].unsqueeze(1).to_broadcast([P, 2, P]), ALU.add)
                v.tensor_tensor(v3[:, 2 * i:2 * i + 2, 1, :], kv[:, :, P:2 * P],
                                bkv1_s[:, P:2 * P].unsqueeze(1).to_broadcast([P, 2, P]), ALU.add).then_inc(l1_kv_stored, 1)

            def add_windows(m, j, i):
                dve.wait_ge(block_summed, 2 * m + i + 1)
                if i:
                    dve.wait_ge(window_added, 4 * m + 2)
                slot = (2 * j + i) * P
                have = mst[:, bass.ds(slot, 2 * P)]
                v.tensor_tensor(have, ps0[:, 0:2 * P], have, ALU.add).then_inc(window_added, 1)
                v.tensor_copy(mst[:, bass.ds(slot + 2 * P, P)], ps0[:, 2 * P:3 * P]).then_inc(window_added, 1)

            def l1_residual(m, par):
                dve.wait_ge(attended, m + 1)
                if not (isinstance(m, int) and m == 0):
                    dve.wait_ge(result_ready, m)
                v.tensor_tensor(t1[:, :], ps0[:, :], tt[:, par, :], ALU.add).then_inc(t1_ready, 1)

            def gate_chain(m, k0):
                def link(ins):
                    ins.then_inc(gate_step, 1)
                    link.k += 1
                    dve.wait_ge(gate_step, GATE_STEPS * m + link.k)
                link.k = k0
                return link

            def gate_logits(m):
                dve.wait_ge(logits_made, m + 1)
                link = gate_chain(m, 0)
                link(v.tensor_tensor(lg[:, :, :], ps2[:, 0:4 * E].rearrange("p (a n) -> p a n", a=4),
                                     rb_s[:, :].unsqueeze(1).to_broadcast([P, 4, E]), ALU.add))
                link(v.tensor_reduce(lm[:, :].unsqueeze(2), lg[:, :, :], AX.X, ALU.max))
                link(v.tensor_tensor(em[:, :, :], lg[:, :, :], lm[:, :].unsqueeze(2).to_broadcast([P, 4, E]),
                                     ALU.subtract))
                grid = [P, 4, E, E]
                other, own = lg[:, :, :].unsqueeze(2).to_broadcast(grid), lg[:, :, :].unsqueeze(3).to_broadcast(grid)
                v.tensor_tensor(above[:, :, :].rearrange("p a (e n) -> p a e n", e=E), other, own, ALU.is_gt)
                last = v.tensor_tensor(equal[:, :, :].rearrange("p a (e n) -> p a e n", e=E), other, own, ALU.is_equal)
                link(last)
                link(v.tensor_tensor(equal[:, :, :], equal[:, :, :],
                                     lower[:, :].unsqueeze(1).to_broadcast([P, 4, E * E]), ALU.mult))
                link(v.tensor_tensor(above[:, :, :], above[:, :, :], equal[:, :, :], ALU.add))
                link(v.tensor_reduce(rank[:, :, :].rearrange("p a n -> p (a n)").unsqueeze(2),
                                     above[:, :, :].rearrange("p a (e n) -> p (a e) n", e=E), AX.X, ALU.add))

            def gate_weights(m):
                dve.wait_ge(exps_made, m + 1)
                link = gate_chain(m, 7)
                link(v.scalar_tensor_tensor(gt[:, :, :], rank[:, :, :], 1.5, ex[:, :, :], ALU.is_lt, ALU.mult))
                link(v.tensor_reduce(es[:, :].unsqueeze(2), gt[:, :, :], AX.X, ALU.add))
                link(v.reciprocal(er[:, :], es[:, :]))
                link(v.tensor_tensor(gt[:, :, :], gt[:, :, :], er[:, :].unsqueeze(2).to_broadcast([P, 4, E]), ALU.mult))
                link(v.tensor_copy(g24[:, :, 0:E], gt[:, :, :]))
                link(v.tensor_tensor(gr[:, :, :], gt[:, :, :], g24[:, :, 0:E], ALU.subtract))
                link(v.tensor_copy(g24[:, :, E:2 * E], gr[:, :, :]))
                v.tensor_tensor(g24[:, :, 2 * E:3 * E], gr[:, :, :], g24[:, :, E:2 * E],
                                ALU.subtract).then_inc(gate_step, 1)
                assert link.k + 1 == GATE_STEPS, link.k

            def gate_input(m, e):
                dve.wait_ge(gate_spread, E * m + e + 1)
                if e >= 2:
                    dve.wait_ge(expert_done, E * m + e - 1)
                v.tensor_tensor(zg[:, e % 2, :], ps2[:, :], z[:, :], ALU.mult).then_inc(gated, 1)

            def result(m):
                dve.wait_ge(expert_done, E * m + E)
                if not (isinstance(m, int) and m == 0):
                    dve.wait_ge(stored, 16 * m)
                v.tensor_tensor(ob[:, :], ps1[:, :], t1[:, :], ALU.add).then_inc(result_ready, 1)

            def side(n, c, par, j):
                if has(n, 1):
                    if j == 2:
                        ln_rsqrt(0, n - 1)
                    if j == 4:
                        ln_scale(0, n - 1, y)
                    if j in (6, 7):
                        l1_keys_values(n - 1, j - 6)
                    if j in (9, 10):
                        add_windows(n - 1, tile_in_image(c, 1), j - 9)
                if has(n, 3):
                    if j == 0:
                        ln_scale(1, n - 3, z)
                    if j == 1:
                        gate_logits(n - 3)
                    if j == 2:
                        gate_weights(n - 3)
                    if 4 <= j < 4 + E:
                        gate_input(n - 3, j - 4)
                    if j == 12:
                        result(n - 3)
                if has(n, 2):
                    if j == 12:
                        l1_residual(n - 2, par)
                    if j == 14:
                        ln_rsqrt(1, n - 2)

            def chunk(b, c, n, par, ahead):
                for j in range(4):
                    shift(n, j)
                    if j == 2 and not (isinstance(c, int) and c == 0):
                        residual(c - 1, n - 1, 1 - par)
                for j in range(NP):
                    if ahead:
                        take_max(n + 1, 2 * j)
                        take_max(n + 1, 2 * j + 1)
                    side(n, c, par, j)
                    if j + 4 < NP:
                        shift(n, j + 4)
                if ahead:
                    fold_max(n + 1)
                invert_sums(n)
                if ahead:
                    query_maxima(n + 1)
                norm_heads(n)
                if not ahead:
                    residual(c, n, par)

            walk(dve, prepare, first_scores, chunk, side)

        @block.tensor
        def _(pe):
            mm = nc.tensor.matmul
            pe.wait_ge(consts_loaded, CONSTS)
            pe.wait_ge(consts_made, 3)

            def prepare(b, n0):
                pe.wait_ge(prep_step, PREP_STEPS * b + 4)
                mm(ps0[:, 0:2], group[:, :], chst[:, :], start=True, stop=True).then_inc(group_summed, 1)
                pe.wait_ge(prep_step, PREP_STEPS * b + H_STEP)
                for t in range(NCH):
                    i = NCH * b + t
                    tile = slice(t * T, (t + 1) * T)
                    if t >= 2:
                        pe.wait_ge(q_stored, i - 1)
                        pe.wait_ge(kv_held, 2 * i - 2)
                    mm(psS[:, t % 2, :], wq_s[:, :], h[:, tile], start=True, stop=True).then_inc(q_made, 1)
                    mm((psS[:, 2, :], psM[:, :])[t % 2], wk_s[:, :], h[:, tile], start=True, stop=True)
                    for u in range(4):
                        last = mm((ps0, ps1)[t % 2][:, u * P:(u + 1) * P], h[:, t * T + u * P:t * T + (u + 1) * P],
                                  wv_s[:, :], start=True, stop=True)
                    last.then_inc(kv_made, 1)
                pe.wait_ge(absmax_taken, b + 1)
                mm(ps0[0:2, 0:P], am2[:, :], ident[:, :], start=True, stop=True).then_inc(absmax_turned, 1)
                pe.wait_ge(prep_step, PREP_STEPS * b + PREP_STEPS - 3)
                mm(ps0[:, 0:2], ones[0:2, :], amd[:, :], start=True, stop=True).then_inc(absmax_shared, 1)

            def scores(n, c, k, after_image=False):
                if k >= SB:
                    pe.wait_ge(max_taken, KT * n + k - SB + 1)
                elif not after_image:
                    pe.wait_ge(max_taken, KT * (n - 1) + KT - (KT - 1 - k) % SB)
                qs = bass.ds(c * T, T)
                key = slice(k * P, (k + 1) * P)
                dst = psS[:, k % SB, :]
                mm(dst, kh[:, key], qh[:, qs], start=True, stop=False)
                mm(dst, kh[:, key], ql[:, qs], start=False, stop=False)
                mm(dst, kl[:, key], qh[:, qs], start=False, stop=True).then_inc(scores_ready, 1)

            def values(n, j):
                pe.wait_ge(probs_ready, NP * n + j + 1)
                if j == 0 and not (isinstance(n, int) and n == 0):
                    pe.wait_ge(heads_copied, n)
                for u in range(2):
                    last = mm(psO[:, :], vs[:, 2 * j + u, :], st[:, j, u * T:(u + 1) * T],
                              start=(j == 0 and u == 0), stop=(j == NP - 1 and u == 1))
                last.then_inc(pv_done, 1)

            def turn_max(n):
                pe.wait_ge(max_folded, n + 1)
                for u in range(4):
                    last = nc.tensor.transpose(ps1[:, u * P:(u + 1) * P], mx[:, u * P:(u + 1) * P], ident[:, :])
                last.then_inc(max_turned, 1)

            def spread_max(n):
                pe.wait_ge(max_diag, n + 1)
                mm(psM[:, :], ones[:, :], dgm[:, :, :].rearrange("p a n -> p (a n)"), start=True,
                   stop=True).then_inc(max_spread, 1)

            def sum_rows(n):
                pe.wait_ge(rows_added, NP * n + NP)
                for u in range(4):
                    last = mm(ps2[:, u:u + 1], rs[:, u * P:(u + 1) * P], ones[:, 0:1], start=True, stop=True)
                last.then_inc(sums_ready, 1)

            def spread_sums(n):
                pe.wait_ge(sums_diag, n + 1)
                mm(ps2[:, :], ones[:, :], dgl[:, :, :].rearrange("p a n -> p (a n)"), start=True,
                   stop=True).then_inc(sums_spread, 1)

            def mix_heads(n):
                pe.wait_ge(heads_normed, n + 1)
                mm(ps1[:, :], wo_s[:, :], osb[:, :], start=True, stop=True).then_inc(heads_mixed, 1)

            def first_scores(b, n0):
                pe.wait_ge(low_parts, 2 * b + 2)
                for k in range(KT):
                    scores(n0, 0, k, True)
                turn_max(n0)
                for k in range(SB):
                    scores(n0 + 1, 1, k)
                spread_max(n0)

            def ln_center(k, m, src, ready):
                pe.wait_ge(ready, m + 1)
                if k == 0 and not (isinstance(m, int) and m < 2):
                    pe.wait_ge(normed[1], m - 1)
                mm(ps0[:, :], center[:, :], src, start=True, stop=True).then_inc(centered[k], 1)

            def ln_variance(k, m):
                pe.wait_ge(squared[k], m + 1)
                for u in range(4):
                    last = mm(ps0[:, u:u + 1], sq[:, u * P:(u + 1) * P], meancol[:, :], start=True, stop=True)
                last.then_inc(var_ready[k], 1)

            def ln_spread_rsqrt(k, m):
                pe.wait_ge(ln_diag[k], m + 1)
                mm(ps0[:, :], ones[:, :], dgn[:, :, :].rearrange("p a n -> p (a n)"), start=True,
                   stop=True).then_inc(ln_spread[k], 1)

            def l1_queries(m):
                pe.wait_ge(normed[0], m + 1)
                mm(ps0[:, :], wq1_s[:, :], y[:, :], start=True, stop=True).then_inc(l1_q_made, 1)

            def l1_keys_values(m, i):
                pe.wait_ge(l1_q_stored, m + 1)
                if i:
                    pe.wait_ge(l1_kv_stored, 2 * m + 1)
                for u in range(2):
                    last = mm(ps0[:, 2 * u * P:2 * (u + 1) * P], y[:, (2 * i + u) * P:(2 * i + u + 1) * P],
                              wkv1_s[:, :], start=True, stop=True)
                last.then_inc(l1_kv_made, 1)

            def l1_block(m, i):
                pe.wait_ge(edges_masked, m + 1)
                if i:
                    pe.wait_ge(window_added, 4 * m + 2)
                for u in range(2):
                    last = mm(ps0[:, 0:3 * P], k3[:, 2 * i + u, :],
                              v3[:, 2 * i + u, :, :].rearrange("p a n -> p (a n)"), start=(u == 0), stop=(u == 1))
                last.then_inc(block_summed, 1)

            def l1_attend(m, par):
                pe.wait_ge(window_scaled, m + 1)
                pe.wait_ge(l1_q_stored, m + 1)
                for i in range(2):
                    last = mm(ps0[:, 2 * i * P:2 * (i + 1) * P], mcur[:, i, :], q1[:, par, 2 * i * P:2 * (i + 1) * P],
                              start=True, stop=True)
                last.then_inc(attended, 1)

            def router(m):
                pe.wait_ge(normed[1], m + 1)
                for u in range(4):
                    last = mm(ps2[:, u * E:(u + 1) * E], z[:, u * P:(u + 1) * P], rw_s[:, :], start=True, stop=True)
                last.then_inc(logits_made, 1)

            def turn_gates(m):
                pe.wait_ge(gate_step, GATE_STEPS * m + GATE_STEPS)
                dst = ps2[0:GPARTS * E, 0:T // 2].bitcast(bf16)
                for u in range(4):
                    last = nc.tensor.transpose(dst[:, u * P:(u + 1) * P], g24[:, u, :], identb[:, :])
                last.then_inc(gates_turned, 1)

            def expert_bias(m):
                pe.wait_ge(gates_stored, 2 * m + 2)
                mm(ps1[:, :], eb_s[:, :], gTf, start=True, stop=False)

            def spread_gate(m, e):
                if e:
                    pe.wait_ge(gated, E * m + e)
                mm(ps2[:, :], sel[:, e, :], gT[:, :], start=True, stop=True).then_inc(gate_spread, 1)

            def expert(m, e):
                pe.wait_ge(gated, E * m + e + 1)
                mm(ps1[:, :], ew_s[:, e, :], zg[:, e % 2, :], start=False, stop=(e == E - 1)).then_inc(expert_done, 1)

            def side(n, c, par, j):
                if has(n, 3):
                    if j == 0:
                        ln_spread_rsqrt(1, n - 3)
                    if j == 1:
                        router(n - 3)
                    if j == 3:
                        turn_gates(n - 3)
                    if j == 4:
                        expert_bias(n - 3)
                        spread_gate(n - 3, 0)
                    if 4 < j < 4 + E:
                        spread_gate(n - 3, j - 4)
                        expert(n - 3, j - 5)
                    if j == 4 + E:
                        expert(n - 3, E - 1)
                if has(n, 1):
                    if j == 1:
                        ln_center(0, n - 1, tt[:, 1 - par, :], layer0_out)
                    if j == 2:
                        ln_variance(0, n - 1)
                    if j == 4:
                        ln_spread_rsqrt(0, n - 1)
                    if j == 5:
                        l1_queries(n - 1)
                    if j in (6, 7):
                        l1_keys_values(n - 1, j - 6)
                    if j in (9, 10):
                        l1_block(n - 1, j - 9)
                if has(n, 2):
                    if j == 12:
                        l1_attend(n - 2, par)
                    if j == 13:
                        ln_center(1, n - 2, t1[:, :], t1_ready)
                    if j == 14:
                        ln_variance(1, n - 2)

            def chunk(b, c, n, par, ahead):
                for j in range(NP):
                    values(n, j)
                    if ahead:
                        for k in (2 * j, 2 * j + 1):
                            if k >= SB:
                                scores(n + 1, c + 1, k)
                    side(n, c, par, j)
                if has(n, 3):
                    pe.wait_ge(result_ready, n - 2)
                sum_rows(n)
                if ahead:
                    turn_max(n + 1)
                if ahead == 2:
                    for k in range(SB):
                        scores(n + 2, c + 2, k)
                if ahead:
                    spread_max(n + 1)
                spread_sums(n)
                mix_heads(n)

            walk(pe, prepare, first_scores, chunk, side)


def kernel(**inputs):
    import numpy as np
    import concourse.bacc as bacc
    from concourse.bass_utils import run_bass_kernel_spmd

    def arr(name):
        return np.ascontiguousarray(inputs[name])

    def col(name):
        return arr(name).reshape(-1, 1)

    def rows(a, n=128):
        return np.ascontiguousarray(np.broadcast_to(a.reshape(1, -1), (n, a.size)))

    x = arr("x")
    b, c, hh, ww = x.shape
    e = inputs["L1_ffn_router_w"].shape[1]
    f = np.float32
    group = np.zeros((c, c), f)
    for g in range(0, c, 4):
        group[g:g + 4, g:g + 4] = 0.25
    center = np.full((c, c), -1.0 / c, f)
    center[np.arange(c), np.arange(c)] = 1.0 - 1.0 / c
    sel = np.zeros((3 * e, e * 128), f)
    lower = np.zeros((e, e), f)
    for i in range(e):
        for part in range(3):
            sel[part * e + i, i * 128:(i + 1) * 128] = 1.0
        lower[i, :i] = 1.0
    edges = np.ones((128, 2, 4), f)
    edges[127, 0, 1::2] = 0.0
    edges[0, 1, 0::2] = 0.0
    w1 = "L1_attn_W"
    arrays = {
        "x_in": x.reshape(b, c, hh * ww),
        "norm_w": col("L0_conv_norm_w"), "norm_b": col("L0_conv_norm_b"),
        "wq": arr("L0_conv_Wq"), "bq": col("L0_conv_bq"),
        "wk": arr("L0_conv_Wk"), "bk": col("L0_conv_bk"),
        "wv": arr("L0_conv_Wv"), "bv_rows": rows(arr("L0_conv_bv")),
        "wo": arr("L0_conv_Wo"), "bo": col("L0_conv_bo"),
        "l1_wqT": np.ascontiguousarray(arr(w1 + "q").T), "l1_bq": col("L1_attn_bq"),
        "l1_wkvT": np.ascontiguousarray(np.concatenate([arr(w1 + "k").T, arr(w1 + "v").T], axis=1)),
        "l1_bkv_rows": rows(np.concatenate([arr("L1_attn_bk"), arr("L1_attn_bv")])),
        "router_w": arr("L1_ffn_router_w"), "router_b_rows": rows(arr("L1_ffn_router_b")),
        "expert_w": arr("L1_ffn_expert_w"),
        "expert_b3": np.ascontiguousarray(np.tile(arr("L1_ffn_expert_b"), (3, 1))),
        "c_ident": np.eye(128, dtype=f), "c_center": center,
        "c_mean": np.full((128, 1), 1.0 / c, f), "c_group": group,
        "c_sel": sel, "c_lower": rows(lower), "c_edges": edges.reshape(128, 8),
    }
    nc = bacc.Bacc("TRN2", target_bir_lowering=False, num_devices=1)
    args = [nc.dram_tensor(n, a.shape, mybir.dt.float32, kind="ExternalInput").ap() for n, a in arrays.items()]
    args.append(nc.dram_tensor("out", (b, c, hh * ww), mybir.dt.float32, kind="ExternalOutput").ap())
    conv_attn_hybrid_kernel(nc, *args)
    r = run_bass_kernel_spmd(nc, [arrays], core_ids=[0])
    return r.results[0]["out"].reshape(b, c, hh, ww)
```

```python
import concourse.bass as bass
from concourse import mybir
from contextlib import ExitStack



def conv_attn_hybrid_kernel(nc, x, norm_w, norm_b, wq, bq, wk, bk, wv, bv_rows, wo, bo,
                            l1_wqT, l1_bq, l1_wkvT, l1_bkv_rows, router_w, router_b_rows,
                            expert_w, expert_b9, c_ident, c_center, c_mean, c_group, c_sel, c_lower,
                            c_edges, out):
    fp32, bf16, fp16, i32 = mybir.dt.float32, mybir.dt.bfloat16, mybir.dt.float16, mybir.dt.int32
    ALU = mybir.AluOpType
    ACT = mybir.ActivationFunctionType
    AX = mybir.AxisListType

    B, C, N = x.shape
    P = 128
    T = 512
    NCH = N // T
    KT = N // P
    GROUP_CH = 4
    NP = KT // 2
    E = router_w.shape[1]
    GPARTS = 3
    GROW = 32
    GROWS = GPARTS * GROW
    NB = N // 256
    GN_EPS = LN_EPS = 1e-5
    XHAT_MAX = float(GROUP_CH * N) ** 0.5
    TOP = 32768.0
    RSQRT_SEED = float(0x5F3759DF)
    RSQRT_STEPS = 16
    LAG = 3
    SETUP_STEPS = 18
    PREP_STEPS = NCH + 23
    GATE_STEPS = 15

    ctx = ExitStack()
    with ctx:
        def sb(name, shape, dt=fp32):
            return ctx.enter_context(nc.sbuf_tensor(name, shape, dt))

        def pb(name, shape):
            return ctx.enter_context(nc.psum_tensor(name, shape, fp32))

        def sem(name):
            return ctx.enter_context(nc.semaphore(name))

        ident = sb("ident", [P, P])
        identb = sb("identb", [P, P], bf16)
        center = sb("center", [P, P])
        meancol = sb("meancol", [P, 1])
        group = sb("group", [P, P])
        ones = sb("ones", [P, P])
        sel = sb("sel", [E * GPARTS, E, P], bf16)
        lower = sb("lower", [P, E * E])
        halves = sb("halves", [P, 4])
        edges = sb("edges", [P, 2, 4])
        wq_s, wk_s, wv_s, wo_s = (sb(n, [P, P]) for n in ("wq_s", "wk_s", "wv_s", "wo_s"))
        wq1_s = sb("wq1_s", [P, P])
        wkv1_s = sb("wkv1_s", [P, 2 * P])
        cols = sb("cols", [P, 6])
        gw_c, gb_c, bq_c, bk_c, bo_c, bq1_c = (cols[:, i:i + 1] for i in range(6))
        bv_s = sb("bv_s", [P, P])
        bkv1_s = sb("bkv1_s", [P, 2 * P])
        rw_s = sb("rw_s", [P, E])
        rb_s = sb("rb_s", [P, E])
        ew_s = sb("ew_s", [P, E, P])
        eb_s = sb("eb_s", [GROWS, P], bf16)
        eb_part = sb("eb_part", [GROWS, P], bf16)

        h = sb("h", [P, N])
        xr = sb("xr", [P, T])
        qh, ql, kh, kl = (sb(n, [P, N], fp16) for n in ("qh", "ql", "kh", "kl"))
        vs = sb("vs", [P, KT, P])
        st = sb("st", [P, NP, 2 * T])
        self32 = st[0:E * GPARTS, NP - 1, 0:E * P]
        eb_rest = st[0:GROWS, NP - 2, 0:P]
        wabs = st[:, 0, 0:2 * P].rearrange("p (a n) -> p a n", a=2)
        bstats = sb("bstats", [P, NCH, 6])
        chst = sb("chst", [P, 2])
        gst = sb("gst", [P, 2])
        gsm = sb("gsm", [P, 8])
        cabs = sb("cabs", [P, 4])
        most = sb("most", [P, 1])
        bound = sb("bound", [P, 2])
        amr = sb("amr", [2, 1])
        amd = sb("amd", [2, 2])
        ag = sb("ag", [P, 2])
        pw = sb("pw", [P, 2])
        ipw = sb("ipw", [P, 2])
        sc = sb("sc", [P, 1])

        acc = sb("acc", [P, T])
        acc_odd = sb("acc_odd", [P, T])
        mq = sb("mq", [P, 4])
        dgm = sb("dgm", [P, 4, P])
        rs = sb("rs", [P, 2 * T])
        rl = sb("rl", [P, 4])
        dgl = sb("dgl", [P, 4, P])
        osb = sb("osb", [P, T])

        tt = sb("tt", [P, 2, T])
        xc = sb("xc", [P, T])
        sq = sb("sq", [P, T])
        rsm = [sb(f"rsm{k}", [P, 4, 4]) for k in range(2)]
        dgn = sb("dgn", [P, 4, P])
        y = sb("y", [P, T])
        z = sb("z", [P, T])
        q1 = sb("q1", [P, 2, T])
        k3 = sb("k3", [P, 4, P])
        v3 = sb("v3", [P, 4, 3, P])
        mst = sb("mst", [P, (NB + 2) * P])
        mcur = sb("mcur", [P, 2, P])
        t1 = sb("t1", [P, 2, T])
        lg, ex, em, gt, gr = (sb(n, [P, 4, E]) for n in ("lg", "ex", "em", "gt", "gr"))
        lm, es, er = (sb(n, [P, 4]) for n in ("lm", "es", "er"))
        rank = sb("rank", [P, 4, E])
        gparts = sb("gparts", [P, 4, GROWS], bf16)
        gT = sb("gT", [GROWS, T], bf16)
        zg = sb("zg", [P, 2, T])
        ob = sb("ob", [P, T])
        above, equal = (ob[:, i * 4 * E * E:(i + 1) * 4 * E * E].rearrange("p (a n) -> p a n", a=4) for i in range(2))

        SB = 3
        psS = pb("psS", [P, SB, T])
        psM = pb("psM", [P, T])
        psO = pb("psO", [P, T])
        ps0 = pb("ps0", [P, T])
        ps1 = pb("ps1", [P, T])
        ps2 = pb("ps2", [P, T])

        consts_loaded, consts_made, x_loaded = sem("consts_loaded"), sem("consts_made"), sem("x_loaded")
        residual_loaded = sem("residual_loaded")
        setup_step, abs_made, bounds_made, bounds_turned, bounds_shared = (
            sem(n) for n in ("setup_step", "abs_made", "bounds_made", "bounds_turned", "bounds_shared"))
        prep_step, group_summed, h_ready = sem("prep_step"), sem("group_summed"), sem("h_ready")
        q_made, k_made, v_made = sem("q_made"), sem("k_made"), sem("v_made")
        high_parts, low_parts, v_stored = sem("high_parts"), sem("low_parts"), sem("v_stored")
        scores_ready, scores_copied, max_taken, shifted = (
            sem(n) for n in ("scores_ready", "scores_copied", "max_taken", "shifted"))
        probs_ready, pv_done, rows_added = sem("probs_ready"), sem("pv_done"), sem("rows_added")
        maxima_joined = sem("maxima_joined")
        max_turned, query_max, max_diag, max_spread = (
            sem(n) for n in ("max_turned", "query_max", "max_diag", "max_spread"))
        sums_ready, sums_inverted, sums_diag, sums_spread = (
            sem(n) for n in ("sums_ready", "sums_inverted", "sums_diag", "sums_spread"))
        heads_copied, heads_normed, heads_mixed, layer0_out = (
            sem(n) for n in ("heads_copied", "heads_normed", "heads_mixed", "layer0_out"))
        centered, center_copied, squared, var_ready, rsqrt_step, ln_diag, ln_spread, normed = (
            [sem(f"{n}{k}") for k in range(2)] for n in
            ("centered", "center_copied", "squared", "var_ready", "rsqrt_step", "ln_diag", "ln_spread", "normed"))
        l1_q_made, l1_q_stored, l1_kv_made, l1_kv_stored, edges_masked, block_summed, window_added = (
            sem(n) for n in ("l1_q_made", "l1_q_stored", "l1_kv_made", "l1_kv_stored", "edges_masked",
                             "block_summed", "window_added"))
        window_scaled, attended, t1_ready, logits_made, gate_step, exps_made = (
            sem(n) for n in ("window_scaled", "attended", "t1_ready", "logits_made", "gate_step", "exps_made"))
        gates_turned, gates_stored, gate_spread, gated, expert_done, result_ready, stored = (
            sem(n) for n in ("gates_turned", "gates_stored", "gate_spread", "gated", "expert_done",
                             "result_ready", "stored"))

        block = ctx.enter_context(nc.Block())

        early = [(cols[:, i:i + 1], a) for i, a in enumerate((norm_w, norm_b, bq, bk, bo, l1_bq))]
        early += [(dst[:, :], src) for dst, src in ((group, c_group), (wq_s, wq), (wk_s, wk), (ident, c_ident))]
        late = [(dst[:, :], src) for dst, src in (
            (wv_s, wv), (bv_s, bv_rows), (center, c_center), (wo_s, wo), (lower, c_lower), (wq1_s, l1_wqT),
            (wkv1_s, l1_wkvT), (bkv1_s, l1_bkv_rows), (rw_s, router_w), (rb_s, router_b_rows),
            (meancol, c_mean))]
        late += [(self32, c_sel), (eb_rest, expert_b9), (edges[:, :, :].rearrange("p a n -> p (a n)"), c_edges),
                 (ew_s[:, :, :], expert_w.rearrange("e d c -> d e c"))]
        CONSTS = 16 * (len(early) + len(late))

        def walk(eng, prepare, first_scores, chunk, step):
            def image(b, n0, first=False, last=False):
                first_scores(b, n0)
                stage = (lambda what: None) if last else (lambda what: what)
                if first:
                    for c in range(NCH - 2):
                        chunk(b, c, c, c % 2, 2, stage("statistics") if c == 1 else None)
                else:
                    chunk(b, 0, n0, 0, 2, None)
                    chunk(b, 1, n0 + 1, 1, 2, stage("statistics"))
                    with eng.Fori(1, NCH // 2 - 1) as twos:
                        c = twos * 2
                        chunk(b, c, n0 + c, 0, 2, None)
                        chunk(b, c + 1, n0 + c + 1, 1, 2, None)
                chunk(b, NCH - 2, n0 + NCH - 2, 0, 1, stage("normalise"))
                chunk(b, NCH - 1, n0 + NCH - 1, 1, 0, stage("project"))
            prepare()
            image(0, 0, first=True)
            with eng.Fori(1, B - 1) as b:
                image(b, b * NCH)
            image(B - 1, (B - 1) * NCH, last=True)
            for n in range(B * NCH, B * NCH + LAG + 1):
                for j in range(-1, NP + 1):
                    step(n, n % NCH, n % 2, j)

        def has(n, lag):
            return not isinstance(n, int) or lag <= n < B * NCH + lag

        def parts(n, j):
            return (NP + 1) * n + j + 1 + (j > 0)

        GATE_STEP = 7

        def score_bank(k, first):
            return psO[:, :] if first and k % (SB + 1) == SB else psS[:, k % (SB + 1 if first else SB), :]

        def attend_step(n):
            return 2 if isinstance(n, int) and n == B * NCH + 1 else 13

        def tile_in_image(c, back):
            return (c - back) % NCH if isinstance(c, int) else c - back

        @block.sync
        def _(sp):
            def load_x(b, t):
                tile = slice(t * T, (t + 1) * T)
                sp.dma_start(h[:, tile], x[bass.ds(b, 1), :, tile].rearrange("a c n -> (a c) n")).then_inc(x_loaded, 16)

            def next_x(b):
                for t in range(NCH):
                    sp.wait_ge(v_made, NCH * (b - 1) + t + 1)
                    load_x(b, t)

            def load_residual(n, b, c):
                if not (isinstance(n, int) and n == 0):
                    sp.wait_ge(layer0_out, n)
                sp.dma_start(xr[:, :], x[bass.ds(b, 1), :, c * T:(c + 1) * T].rearrange("a c n -> (a c) n")
                             ).then_inc(residual_loaded, 16)

            def store(m, b, j):
                sp.wait_ge(result_ready, m + 1)
                sp.dma_start(out[bass.ds(b, 1), :, j * T:(j + 1) * T].rearrange("a c n -> (a c) n"),
                             ob[:, :]).then_inc(stored, 16)

            for t in range(NCH):
                load_x(0, t)
            for dst, src in early:
                sp.dma_start(dst, src).then_inc(consts_loaded, 16)
            next_x(1)

            def image(b, n0, first=False, last=False):
                for c in range(NCH):
                    load_residual(n0 + c, b, c)
                    if not first or c >= LAG:
                        store(n0 + c - LAG, b if c >= LAG else b - 1, (c - LAG) % NCH)
                if not last:
                    next_x(b + 2)

            image(0, 0, first=True)
            with sp.Fori(1, B - 2) as b:
                image(b, b * NCH)
            for b in range(B - 2, B):
                image(b, b * NCH, last=True)
            for m in range(B * NCH - LAG, B * NCH):
                store(m, m // NCH, m % NCH)
            sp.wait_ge(stored, 16 * B * NCH)

        def rsqrt_seed(eng, s, step, base, k):
            eng.tensor_scalar(s[1].bitcast(i32), s[0].bitcast(i32), 1, None, ALU.logical_shift_right).then_inc(step, 1)
            eng.wait_ge(step, base + k + 1)
            eng.tensor_scalar(s[3].bitcast(i32), s[1].bitcast(i32), -1.0, RSQRT_SEED, ALU.mult, ALU.add).then_inc(step, 1)
            eng.tensor_scalar(s[0], s[0], -0.5, None, ALU.mult).then_inc(step, 1)
            return k + 3

        def rsqrt_newton(eng, s, step, base, k, halves):
            for _ in range(3):
                eng.wait_ge(step, base + k)
                eng.tensor_tensor(s[1], s[3], s[3], ALU.mult).then_inc(step, 1)
                eng.wait_ge(step, base + k + 1)
                eng.tensor_tensor(s[2], s[1], s[0], ALU.mult).then_inc(step, 1)
                eng.wait_ge(step, base + k + 2)
                eng.tensor_tensor(s[1], s[2], halves, ALU.add).then_inc(step, 1)
                eng.wait_ge(step, base + k + 3)
                eng.tensor_tensor(s[3], s[3], s[1], ALU.mult).then_inc(step, 1)
                k += 4
            return k

        @block.gpsimd
        def _(pool):
            nc.gpsimd.memset(ones[:, :], 1.0).then_inc(consts_made, 1)
            nc.gpsimd.memset(halves[:, :], 1.5).then_inc(consts_made, 1)

            def ln_rsqrt(k, m):
                s = [rsm[k][:, i, :] for i in range(4)]
                assert rsqrt_newton(nc.gpsimd, s, rsqrt_step[k], RSQRT_STEPS * m, 4, halves[:, :]) == RSQRT_STEPS
                pool.wait_ge(rsqrt_step[k], RSQRT_STEPS * m + RSQRT_STEPS)
                if not (isinstance(m, int) and m == 0):
                    pool.wait_ge(ln_spread[k], m)
                nc.gpsimd.tensor_tensor(dgn[:, :, :], ident[:, :].unsqueeze(1).to_broadcast([P, 4, P]),
                                        rsm[k][:, 3, :].unsqueeze(2).to_broadcast([P, 4, P]),
                                        ALU.mult).then_inc(ln_diag[k], 1)

            def add_rows(n, j):
                pool.wait_ge(probs_ready, parts(n, j))
                if j == 1:
                    if not (isinstance(n, int) and n == 0):
                        pool.wait_ge(sums_ready, n)
                    a = st[:, 0, :]
                else:
                    pool.wait_ge(rows_added, NP * n + j - 1)
                    a = rs[:, :]
                nc.gpsimd.tensor_tensor(rs[:, :], a, st[:, j, :], ALU.add).then_inc(rows_added, 1)

            def fold_rows(n):
                pool.wait_ge(rows_added, NP * n + NP - 1)
                nc.gpsimd.tensor_tensor(rs[:, 0:T], rs[:, 0:T], rs[:, T:2 * T], ALU.add).then_inc(rows_added, 1)

            def mask_edges(m):
                pool.wait_ge(l1_kv_stored, 2 * m + 2)
                for s in (0, 1):
                    last = nc.gpsimd.tensor_tensor(v3[:, :, 2 * s, :], v3[:, :, 1, :],
                                                   edges[:, s, :].unsqueeze(2).to_broadcast([P, 4, P]), ALU.mult)
                last.then_inc(edges_masked, 1)

            def side(n, c, par, j):
                if j == 4 and has(n, 1):
                    ln_rsqrt(0, n - 1)
                if j == 9 and has(n, 1):
                    mask_edges(n - 1)
                if j == 0 and has(n, 3):
                    ln_rsqrt(1, n - 3)

            def chunk(b, c, n, par, ahead, stage):
                for j in range(NP):
                    if j:
                        add_rows(n, j)
                    side(n, c, par, j)
                fold_rows(n)

            pool.wait_ge(consts_loaded, CONSTS)
            pool.wait_ge(consts_made, 4)
            walk(pool, lambda: None, lambda b, n0: None, chunk, side)

        @block.scalar
        def _(act):
            for dst, src in late:
                act.dma_start(dst, src).then_inc(consts_loaded, 16)
            act.wait_ge(consts_loaded, CONSTS)
            nc.scalar.activation(sel[:, :, :].rearrange("p a n -> p (a n)"), self32, ACT.Copy).then_inc(consts_made, 1)
            nc.scalar.activation(identb[:, :], ident[:, :], ACT.Copy).then_inc(consts_made, 1)

            nc.scalar.activation(wabs[:, 0, :], wq_s[:, :], ACT.Abs).then_inc(abs_made, 1)
            nc.scalar.activation(wabs[:, 1, :], wk_s[:, :], ACT.Abs).then_inc(abs_made, 1)
            nc.scalar.activation(cabs[:, :], cols[:, 0:4], ACT.Abs).then_inc(abs_made, 1)
            act.wait_ge(setup_step, SETUP_STEPS)

            def normalise(b, t):
                if t == 0:
                    act.wait_ge(prep_step, PREP_STEPS * b + PREP_STEPS)
                tile = h[:, t * T:(t + 1) * T]
                nc.scalar.activation(tile, tile, ACT.Identity, bias=gsm[:, 6:7], scale=gsm[:, 5:6]).then_inc(h_ready, 1)

            def high_part(b, t, dst, made, bank, bias):
                act.wait_ge(made, NCH * b + t + 1)
                nc.scalar.activation(dst[:, t * T:(t + 1) * T], psS[:, bank, :], ACT.Identity,
                                     bias=bias).then_inc(high_parts, 1)

            def prepare():
                for t in range(NCH):
                    normalise(0, t)
                    if t:
                        high_part(0, t - 1, kh, k_made, 0, bk_c)
                        high_part(0, t - 1, qh, q_made, 1, bq_c)
                high_part(0, NCH - 1, kh, k_made, 0, bk_c)
                high_part(0, NCH - 1, qh, q_made, 1, bq_c)

            def copy_scores(n, k, first=False):
                act.wait_ge(max_taken, KT * n + k + 1)
                if not (isinstance(n, int) and n == 0):
                    act.wait_ge(pv_done, NP * (n - 1) + k // 2 + 1)
                    act.wait_ge(rows_added, NP * (n - 1) + max(k // 2, 1))
                nc.scalar.activation(st[:, k // 2, (k % 2) * T:(k % 2 + 1) * T], score_bank(k, first),
                                     ACT.Copy).then_inc(scores_copied, 1)

            def exponentiate(n, j):
                for half in ((slice(0, T), slice(T, 2 * T)) if j == 0 else (slice(0, 2 * T),)):
                    act.wait_ge(shifted, parts(n, j) + (half.start > 0))
                    nc.scalar.activation(st[:, j, half], st[:, j, half], ACT.Exp, scale=sc[:, :]).then_inc(probs_ready, 1)

            def first_scores(b, n0):
                for k in range(KT):
                    copy_scores(n0, k, True)

            def ln_center(k, m):
                act.wait_ge(centered[k], m + 1)
                nc.scalar.activation(xc[:, :], ps0[:, :], ACT.Copy).then_inc(center_copied[k], 1)
                act.wait_ge(center_copied[k], m + 1)
                nc.scalar.activation(sq[:, :], xc[:, :], ACT.Square).then_inc(squared[k], 1)

            def l1_query(m, par):
                act.wait_ge(l1_q_made, m + 1)
                nc.scalar.activation(q1[:, par, :], ps0[:, :], ACT.Identity, bias=bq1_c).then_inc(l1_q_stored, 1)

            def scale_window(m, j, tiles_added):
                act.wait_ge(window_added, 4 * tiles_added)
                nc.scalar.activation(mcur[:, :, :].rearrange("p a n -> p (a n)"),
                                     mst[:, bass.ds((2 * j + 1) * P, 2 * P)], ACT.Copy,
                                     scale=float(C) ** -0.5).then_inc(window_scaled, 1)

            def exp_logits(m):
                act.wait_ge(gate_step, GATE_STEPS * m + 3)
                nc.scalar.activation(ex[:, :, :], em[:, :, :], ACT.Exp).then_inc(exps_made, 1)

            def store_gates(m):
                act.wait_ge(gates_turned, m + 1)
                nc.scalar.activation(gT[:, :], ps2[0:GROWS, 0:T // 2].bitcast(bf16), ACT.Copy).then_inc(gates_stored, 1)

            def copy_heads(n):
                act.wait_ge(pv_done, NP * n + NP)
                nc.scalar.activation(osb[:, :], psO[:, :], ACT.Copy).then_inc(heads_copied, 1)

            def side(n, c, par, j):
                if has(n, 1):
                    if j == 2:
                        ln_center(0, n - 1)
                    if j == 6:
                        l1_query(n - 1, 1 - par)
                if has(n, 2):
                    if j == attend_step(n) - 1:
                        scale_window(n - 2, tile_in_image(c, 2), min(n, B * NCH) if isinstance(n, int) else n)
                    if j == attend_step(n) + 1:
                        ln_center(1, n - 2)
                if has(n, 3):
                    if j == 2:
                        exp_logits(n - 3)
                    if j == GATE_STEP - 2:
                        store_gates(n - 3)

            def chunk(b, c, n, par, ahead, stage):
                exponentiate(n, 0)
                exponentiate(n, 1)
                for j in range(NP):
                    if ahead:
                        copy_scores(n + 1, 2 * j)
                        copy_scores(n + 1, 2 * j + 1)
                    if j + 2 < NP:
                        exponentiate(n, j + 2)
                    side(n, c, par, j)
                    if stage == "normalise" and 4 <= j < 4 + NCH:
                        normalise(b + 1, j - 4)
                    if stage == "project" and j % 2 == 0:
                        high_part(b + 1, j // 2, kh, k_made, 0, bk_c)
                        high_part(b + 1, j // 2, qh, q_made, 1, bq_c)
                copy_heads(n)

            walk(act, prepare, first_scores, chunk, side)

        @block.vector
        def _(dve):
            v = nc.vector

            def setup():
                k = 0

                def link(ins):
                    nonlocal k
                    ins.then_inc(setup_step, 1)
                    k += 1
                    dve.wait_ge(setup_step, k)

                dve.wait_ge(abs_made, 3)
                link(v.scalar_tensor_tensor(most[:, :], cabs[:, 0:1], XHAT_MAX, cabs[:, 1:2], ALU.mult, ALU.add))
                dve.wait_ge(bounds_made, 1)
                link(v.tensor_tensor(bound[:, :], ps0[:, 0:2], cabs[:, 2:4], ALU.add))
                dve.wait_ge(bounds_turned, 1)
                link(v.tensor_reduce(amr[:, :], ps0[0:2, 0:P], AX.X, ALU.max))
                link(v.tensor_scalar(amd[:, :], ident[0:2, 0:2], amr[:, :], None, ALU.mult))
                dve.wait_ge(bounds_shared, 1)
                link(v.tensor_scalar(ag[:, :], ps0[:, 0:2], 1e-15, 1.0 / TOP, ALU.max, ALU.mult))
                link(v.reciprocal(ipw[:, :], ag[:, :]))
                link(v.tensor_scalar(pw[:, :].bitcast(i32), ipw[:, :].bitcast(i32), 0x7F800000, None, ALU.bitwise_and))
                link(v.reciprocal(ipw[:, :], pw[:, :]))
                link(v.tensor_scalar(sc[:, :], ipw[:, 0:1], ipw[:, 1:2], float(C) ** -0.5, ALU.mult, ALU.mult))
                link(v.tensor_scalar(wq_s[:, :], wq_s[:, :], pw[:, 0:1], None, ALU.mult))
                link(v.tensor_scalar(wk_s[:, :], wk_s[:, :], pw[:, 1:2], None, ALU.mult))
                link(v.tensor_scalar(bq_c, bq_c, pw[:, 0:1], None, ALU.mult))
                link(v.tensor_scalar(bk_c, bk_c, pw[:, 1:2], None, ALU.mult))
                link(v.tensor_copy(eb_s[:, :], eb_rest))
                link(v.tensor_tensor(eb_rest, eb_rest, eb_s[:, :], ALU.subtract))
                link(v.tensor_copy(eb_part[:, :], eb_rest))
                link(v.tensor_tensor(eb_rest, eb_rest, eb_part[:, :], ALU.subtract))
                v.tensor_copy(eb_s[GROW:2 * GROW, :], eb_part[GROW:2 * GROW, :])
                v.memset(gparts[:, :, :], 0.0)
                link(v.tensor_copy(eb_s[2 * GROW:GROWS, :], eb_rest[2 * GROW:GROWS, :]))
                assert k == SETUP_STEPS, k

            def clear_window():
                v.memset(mst[:, 0:2 * P], 0.0)

            def prep_chain(b, k0):
                def link(ins):
                    ins.then_inc(prep_step, 1)
                    link.k += 1
                    dve.wait_ge(prep_step, PREP_STEPS * b + link.k)
                link.k = k0
                return link

            def tile_statistics(b, t):
                if t == 0:
                    dve.wait_ge(x_loaded, 16 * NCH * (b + 1))
                v.bn_stats(bstats[:, t, :], h[:, t * T:(t + 1) * T]).then_inc(prep_step, 1)

            def channel_statistics(b):
                dve.wait_ge(prep_step, PREP_STEPS * b + NCH)
                v.memset(gsm[:, 7:8], 0.0)
                link = prep_chain(b, NCH)
                link(v.bn_aggr(chst[:, :], bstats[:, :, :].rearrange("p a n -> p (a n)")))
                v.scalar_tensor_tensor(chst[:, 1:2], chst[:, 0:1], chst[:, 0:1], chst[:, 1:2], ALU.mult,
                                       ALU.add).then_inc(prep_step, 1)

            def copy_group_statistics(b):
                dve.wait_ge(group_summed, b + 1)
                v.tensor_copy(gst[:, :], ps2[:, 0:2]).then_inc(prep_step, 1)

            def group_norm(b):
                dve.wait_ge(prep_step, PREP_STEPS * b + NCH + 3)
                link = prep_chain(b, NCH + 3)
                s = [gsm[:, i:i + 1] for i in range(8)]
                link(v.scalar_tensor_tensor(s[4], gst[:, 0:1], gst[:, 0:1], gst[:, 1:2], ALU.mult, ALU.subtract))
                link(v.tensor_scalar(s[0], s[4], -1.0, GN_EPS, ALU.mult, ALU.add))
                link.k = rsqrt_seed(v, s, prep_step, PREP_STEPS * b, link.k)
                link.k = rsqrt_newton(v, s, prep_step, PREP_STEPS * b, link.k, halves[:, 0:1])
                dve.wait_ge(prep_step, PREP_STEPS * b + link.k)
                link(v.tensor_tensor(s[5], s[3], gw_c, ALU.mult))
                link(v.scalar_tensor_tensor(s[4], gst[:, 0:1], s[5], gb_c, ALU.mult, ALU.subtract))
                v.tensor_scalar(s[6], s[4], -1.0, None, ALU.mult).then_inc(prep_step, 1)
                assert link.k + 1 == PREP_STEPS, link.k

            def low_part(b, t, i, dst, high, bank, bias):
                tile = slice(t * T, (t + 1) * T)
                dve.wait_ge(high_parts, 2 * (NCH * b + t) + i + 1)
                v.scalar_tensor_tensor(dst[:, tile], psS[:, bank, :], bias, high[:, tile], ALU.add,
                                       ALU.subtract).then_inc(low_parts, 1)

            def store_values(b, t):
                dve.wait_ge(v_made, NCH * b + t + 1)
                v.tensor_tensor(vs[:, 4 * t:4 * t + 4, :], psS[:, 2, :].rearrange("p (a n) -> p a n", a=4),
                                bv_s[:, :].unsqueeze(1).to_broadcast([P, 4, P]), ALU.add).then_inc(v_stored, 1)

            def low_parts_of(b, t):
                low_part(b, t, 0, kl, kh, 0, bk_c)
                low_part(b, t, 1, ql, qh, 1, bq_c)

            def prepare():
                clear_window()
                for t in range(NCH):
                    tile_statistics(0, t)
                channel_statistics(0)
                dve.wait_ge(consts_loaded, CONSTS)
                dve.wait_ge(consts_made, 4)
                setup()
                copy_group_statistics(0)
                group_norm(0)
                for t in range(NCH):
                    low_parts_of(0, t)
                    store_values(0, t)

            def take_max(n, k, first=False):
                dve.wait_ge(scores_ready, KT * n + k + 1)
                run = 2 if first else 1
                dst = (acc, acc_odd)[k % run]
                if k < run:
                    v.tensor_copy(dst[:, :], score_bank(k, first)).then_inc(max_taken, 1)
                else:
                    dve.wait_ge(max_taken, KT * n + k + 1 - run)
                    v.tensor_tensor(dst[:, :], score_bank(k, first), dst[:, :], ALU.max).then_inc(max_taken, 1)

            def join_maxima(n):
                dve.wait_ge(max_taken, KT * n + KT)
                v.tensor_tensor(acc[:, :], acc[:, :], acc_odd[:, :], ALU.max).then_inc(maxima_joined, 1)

            def diagonal(dst, col):
                return v.tensor_tensor(dst[:, :, :], ident[:, :].unsqueeze(1).to_broadcast([P, 4, P]),
                                       col.unsqueeze(2).to_broadcast([P, 4, P]), ALU.mult)

            def query_maxima(n):
                dve.wait_ge(max_turned, n + 1)
                v.tensor_reduce(mq[:, :].unsqueeze(2), psM[:, :].rearrange("p (a n) -> p a n", a=4), AX.X,
                                ALU.max).then_inc(query_max, 1)
                dve.wait_ge(query_max, n + 1)
                if not (isinstance(n, int) and n == 0):
                    dve.wait_ge(max_spread, n)
                diagonal(dgm, mq[:, :]).then_inc(max_diag, 1)

            def invert_sums(n):
                dve.wait_ge(sums_ready, n + 1)
                v.reciprocal(rl[:, :], ps2[:, 0:4]).then_inc(sums_inverted, 1)
                dve.wait_ge(sums_inverted, n + 1)
                if not (isinstance(n, int) and n == 0):
                    dve.wait_ge(sums_spread, n)
                diagonal(dgl, rl[:, :]).then_inc(sums_diag, 1)

            def norm_heads(n):
                dve.wait_ge(sums_spread, n + 1)
                dve.wait_ge(heads_copied, n + 1)
                v.tensor_tensor(osb[:, :], ps2[:, :], osb[:, :], ALU.mult).then_inc(heads_normed, 1)

            def residual(n, par):
                dve.wait_ge(heads_mixed, n + 1)
                dve.wait_ge(residual_loaded, 16 * (n + 1))
                v.scalar_tensor_tensor(tt[:, par, :], ps1[:, :], bo_c, xr[:, :], ALU.add,
                                       ALU.add).then_inc(layer0_out, 1)

            def shift(n, j):
                if j == 0:
                    dve.wait_ge(max_spread, n + 1)
                dve.wait_ge(scores_copied, KT * n + 2 * j + 2)
                if j == 0:
                    for half in (st[:, 0, 0:T], st[:, 0, T:2 * T]):
                        v.tensor_tensor(half, half, psM[:, :], ALU.subtract).then_inc(shifted, 1)
                    return
                pair = st[:, j, :].rearrange("p (a n) -> p a n", a=2)
                v.tensor_tensor(pair, pair, psM[:, :].unsqueeze(1).to_broadcast([P, 2, T]),
                                ALU.subtract).then_inc(shifted, 1)

            def first_scores(b, n0):
                for k in range(KT):
                    take_max(n0, k, True)
                join_maxima(n0)
                query_maxima(n0)
                take_max(n0 + 1, 0)

            def ln_variance(k, m):
                dve.wait_ge(var_ready[k], m + 1)
                s = [rsm[k][:, i, :] for i in range(4)]
                v.tensor_scalar(s[0], ps0[:, 0:4], LN_EPS, None, ALU.add).then_inc(rsqrt_step[k], 1)
                dve.wait_ge(rsqrt_step[k], RSQRT_STEPS * m + 1)
                rsqrt_seed(v, s, rsqrt_step[k], RSQRT_STEPS * m, 1)

            def ln_scale(k, m, dst):
                dve.wait_ge(ln_spread[k], m + 1)
                v.tensor_tensor(dst[:, :], ps0[:, :], xc[:, :], ALU.mult).then_inc(normed[k], 1)

            def l1_keys_values(m, i):
                dve.wait_ge(l1_kv_made, 2 * m + i + 1)
                kv = ps0[:, :].rearrange("p (a n) -> p a n", a=2)
                v.tensor_tensor(k3[:, 2 * i:2 * i + 2, :], kv[:, :, 0:P],
                                bkv1_s[:, 0:P].unsqueeze(1).to_broadcast([P, 2, P]), ALU.add)
                v.tensor_tensor(v3[:, 2 * i:2 * i + 2, 1, :], kv[:, :, P:2 * P],
                                bkv1_s[:, P:2 * P].unsqueeze(1).to_broadcast([P, 2, P]), ALU.add).then_inc(l1_kv_stored, 1)

            def add_windows(m, j, i):
                dve.wait_ge(block_summed, 2 * m + i + 1)
                if i:
                    dve.wait_ge(window_added, 4 * m + 2)
                slot = (2 * j + i) * P
                have = mst[:, bass.ds(slot, 2 * P)]
                v.tensor_tensor(have, ps0[:, 0:2 * P], have, ALU.add).then_inc(window_added, 1)
                v.tensor_copy(mst[:, bass.ds(slot + 2 * P, P)], ps0[:, 2 * P:3 * P]).then_inc(window_added, 1)

            def l1_residual(m, par):
                dve.wait_ge(attended, m + 1)
                v.tensor_tensor(t1[:, par, :], ps0[:, :], tt[:, par, :], ALU.add).then_inc(t1_ready, 1)

            def gate_chain(m, k0):
                def link(ins):
                    ins.then_inc(gate_step, 1)
                    link.k += 1
                    dve.wait_ge(gate_step, GATE_STEPS * m + link.k)
                link.k = k0
                return link

            def gate_logits(m):
                dve.wait_ge(logits_made, m + 1)
                link = gate_chain(m, 0)
                link(v.tensor_tensor(lg[:, :, :], ps2[:, 0:4 * E].rearrange("p (a n) -> p a n", a=4),
                                     rb_s[:, :].unsqueeze(1).to_broadcast([P, 4, E]), ALU.add))
                link(v.tensor_reduce(lm[:, :].unsqueeze(2), lg[:, :, :], AX.X, ALU.max))
                v.tensor_tensor(em[:, :, :], lg[:, :, :], lm[:, :].unsqueeze(2).to_broadcast([P, 4, E]),
                                ALU.subtract).then_inc(gate_step, 1)

            def gate_ranks(m):
                if not (isinstance(m, int) and m == 0):
                    dve.wait_ge(stored, 16 * m)
                link = gate_chain(m, 3)
                grid = [P, 4, E, E]
                other, own = lg[:, :, :].unsqueeze(2).to_broadcast(grid), lg[:, :, :].unsqueeze(3).to_broadcast(grid)
                v.tensor_tensor(above[:, :, :].rearrange("p a (e n) -> p a e n", e=E), other, own, ALU.is_gt)
                last = v.tensor_tensor(equal[:, :, :].rearrange("p a (e n) -> p a e n", e=E), other, own, ALU.is_equal)
                link(last)
                link(v.tensor_tensor(equal[:, :, :], equal[:, :, :],
                                     lower[:, :].unsqueeze(1).to_broadcast([P, 4, E * E]), ALU.mult))
                link(v.tensor_tensor(above[:, :, :], above[:, :, :], equal[:, :, :], ALU.add))
                v.tensor_reduce(rank[:, :, :].rearrange("p a n -> p (a n)").unsqueeze(2),
                                above[:, :, :].rearrange("p a (e n) -> p (a e) n", e=E), AX.X,
                                ALU.add).then_inc(gate_step, 1)

            def gate_weights(m):
                dve.wait_ge(exps_made, m + 1)
                dve.wait_ge(gate_step, GATE_STEPS * m + 7)
                link = gate_chain(m, 7)
                link(v.scalar_tensor_tensor(gt[:, :, :], rank[:, :, :], 1.5, ex[:, :, :], ALU.is_lt, ALU.mult))
                link(v.tensor_reduce(es[:, :].unsqueeze(2), gt[:, :, :], AX.X, ALU.add))
                link(v.reciprocal(er[:, :], es[:, :]))
                link(v.tensor_tensor(gt[:, :, :], gt[:, :, :], er[:, :].unsqueeze(2).to_broadcast([P, 4, E]), ALU.mult))
                part = [gparts[:, :, :].rearrange("p a (r n) -> p a r n", n=GROW)[:, :, :, q * E:(q + 1) * E]
                        for q in range(GPARTS)]
                thrice = [P, 4, GPARTS, E]
                link(v.tensor_copy(part[0], gt[:, :, :].unsqueeze(2).to_broadcast(thrice)))
                link(v.tensor_tensor(gr[:, :, :], gt[:, :, :], gparts[:, :, 0:E], ALU.subtract))
                link(v.tensor_copy(part[1], gr[:, :, :].unsqueeze(2).to_broadcast(thrice)))
                v.tensor_tensor(part[2], gr[:, :, :].unsqueeze(2).to_broadcast(thrice),
                                gparts[:, :, E:2 * E].unsqueeze(2).to_broadcast(thrice), ALU.subtract).then_inc(gate_step, 1)
                assert link.k + 1 == GATE_STEPS, link.k

            def gate_input(m, e):
                dve.wait_ge(gate_spread, E * m + e + 1)
                if e >= 2:
                    dve.wait_ge(expert_done, E * m + e - 1)
                v.tensor_tensor(zg[:, e % 2, :], ps2[:, :], z[:, :], ALU.mult).then_inc(gated, 1)

            def result(m, par):
                dve.wait_ge(expert_done, E * m + E)
                v.tensor_tensor(ob[:, :], ps1[:, :], t1[:, par, :], ALU.add).then_inc(result_ready, 1)

            def side(n, c, par, j):
                if has(n, 3) and GATE_STEP <= j < GATE_STEP + E:
                    gate_input(n - 3, j - GATE_STEP)
                if has(n, 4) and j == 0:
                    result(n - 4, par)
                if has(n, 1):
                    if j == -1:
                        invert_sums(n - 1)
                    if j == 0:
                        norm_heads(n - 1)
                    if j == 1:
                        residual(n - 1, 1 - par)
                    if j == 3:
                        ln_variance(0, n - 1)
                    if j == 5:
                        ln_scale(0, n - 1, y)
                    if j in (7, 8):
                        l1_keys_values(n - 1, j - 7)
                    if j in (10, 11):
                        add_windows(n - 1, tile_in_image(c, 1), j - 10)
                if has(n, 3):
                    if j == 1:
                        ln_scale(1, n - 3, z)
                    if j == 2:
                        gate_logits(n - 3)
                    if j == 3:
                        gate_ranks(n - 3)
                    if j == GATE_STEP - 3:
                        gate_weights(n - 3)
                if has(n, 2):
                    if j == attend_step(n):
                        l1_residual(n - 2, par)
                    if j == attend_step(n) + 3:
                        ln_variance(1, n - 2)

            def chunk(b, c, n, par, ahead, stage):
                shift(n, 0)
                side(n, c, par, -1)
                shift(n, 1)
                if ahead:
                    take_max(n + 1, 1)
                for j in range(NP):
                    if ahead and j:
                        take_max(n + 1, 2 * j)
                        take_max(n + 1, 2 * j + 1)
                    side(n, c, par, j)
                    if j == 0:
                        shift(n, 2)
                    if j + 3 < NP:
                        shift(n, j + 3)
                    if stage == "statistics":
                        if j < NCH:
                            tile_statistics(b + 1, j)
                        if j == NCH:
                            channel_statistics(b + 1)
                        if j == NP - 1:
                            copy_group_statistics(b + 1)
                    if stage == "normalise" and j == 2:
                        group_norm(b + 1)
                    if stage == "project":
                        if j == 0:
                            clear_window()
                        if j % 2 == 0:
                            low_parts_of(b + 1, j // 2)
                        else:
                            store_values(b + 1, j // 2)
                if ahead:
                    query_maxima(n + 1)
                side(n, c, par, NP)
                if ahead == 2:
                    take_max(n + 2, 0)

            walk(dve, prepare, first_scores, chunk, side)

        @block.tensor
        def _(pe):
            mm = nc.tensor.matmul
            pe.wait_ge(consts_loaded, CONSTS)
            pe.wait_ge(consts_made, 4)

            pe.wait_ge(abs_made, 3)
            pe.wait_ge(setup_step, 1)
            for i in range(2):
                last = mm(ps0[:, i:i + 1], wabs[:, i, :], most[:, :], start=True, stop=True)
            last.then_inc(bounds_made, 1)
            pe.wait_ge(setup_step, 2)
            mm(ps0[0:2, 0:P], bound[:, :], ident[:, :], start=True, stop=True).then_inc(bounds_turned, 1)
            pe.wait_ge(setup_step, 4)
            mm(ps0[:, 0:2], ones[0:2, :], amd[:, :], start=True, stop=True).then_inc(bounds_shared, 1)
            pe.wait_ge(setup_step, SETUP_STEPS)

            def group_statistics(b, n):
                if has(n, LAG):
                    pe.wait_ge(gated, E * (n - LAG + 1))
                pe.wait_ge(prep_step, PREP_STEPS * b + NCH + 2)
                mm(ps2[:, 0:2], group[:, :], chst[:, :], start=True, stop=True).then_inc(group_summed, 1)

            def project_keys_queries(b, t):
                i = NCH * b + t
                tile = slice(t * T, (t + 1) * T)
                pe.wait_ge(h_ready, i + 1)
                if t:
                    pe.wait_ge(low_parts, 2 * i - 1)
                mm(psS[:, 0, :], wk_s[:, :], h[:, tile], start=True, stop=True).then_inc(k_made, 1)
                if t:
                    pe.wait_ge(low_parts, 2 * i)
                mm(psS[:, 1, :], wq_s[:, :], h[:, tile], start=True, stop=True).then_inc(q_made, 1)

            def project_values(b, t):
                if t:
                    pe.wait_ge(v_stored, NCH * b + t)
                for u in range(4):
                    last = mm(psS[:, 2, u * P:(u + 1) * P], h[:, t * T + u * P:t * T + (u + 1) * P],
                              wv_s[:, :], start=True, stop=True)
                last.then_inc(v_made, 1)

            def prepare():
                group_statistics(0, 0)
                for t in range(NCH):
                    project_keys_queries(0, t)
                    project_values(0, t)

            def scores(n, c, k, first=False, second=False):
                banks = SB + first
                if k >= banks:
                    pe.wait_ge(scores_copied, KT * n + k - banks + 1)
                elif second:
                    pe.wait_ge(scores_copied, KT * (n - 1) + KT - SB + k)
                elif not first:
                    pe.wait_ge(scores_copied, KT * (n - 1) + KT - (KT - 1 - k) % SB)
                qs = bass.ds(c * T, T)
                key = slice(k * P, (k + 1) * P)
                dst = score_bank(k, first)
                mm(dst, kh[:, key], qh[:, qs], start=True, stop=False)
                mm(dst, kh[:, key], ql[:, qs], start=False, stop=False)
                mm(dst, kl[:, key], qh[:, qs], start=False, stop=True).then_inc(scores_ready, 1)

            def values(n, j):
                pe.wait_ge(probs_ready, parts(n, j))
                if j == 0 and not (isinstance(n, int) and n == 0):
                    pe.wait_ge(heads_copied, n)
                for u in range(2):
                    if j == 0 and u == 1:
                        pe.wait_ge(probs_ready, parts(n, 0) + 1)
                    last = mm(psO[:, :], vs[:, 2 * j + u, :], st[:, j, u * T:(u + 1) * T],
                              start=(j == 0 and u == 0), stop=(j == NP - 1 and u == 1))
                last.then_inc(pv_done, 1)

            def turn_max(n):
                pe.wait_ge(max_taken, KT * n + KT)
                for u in range(4):
                    last = nc.tensor.transpose(psM[:, u * P:(u + 1) * P], acc[:, u * P:(u + 1) * P], ident[:, :])
                last.then_inc(max_turned, 1)

            def spread_max(n):
                pe.wait_ge(max_diag, n + 1)
                mm(psM[:, :], ones[:, :], dgm[:, :, :].rearrange("p a n -> p (a n)"), start=True,
                   stop=True).then_inc(max_spread, 1)

            def sum_rows(n):
                pe.wait_ge(rows_added, NP * n + NP)
                if has(n, LAG):
                    pe.wait_ge(gated, E * (n - LAG + 1))
                for u in range(4):
                    last = mm(ps2[:, u:u + 1], rs[:, u * P:(u + 1) * P], ones[:, 0:1], start=True, stop=True)
                last.then_inc(sums_ready, 1)

            def spread_sums(n):
                pe.wait_ge(sums_diag, n + 1)
                mm(ps2[:, :], ones[:, :], dgl[:, :, :].rearrange("p a n -> p (a n)"), start=True,
                   stop=True).then_inc(sums_spread, 1)

            def mix_heads(n):
                pe.wait_ge(heads_normed, n + 1)
                mm(ps1[:, :], wo_s[:, :], osb[:, :], start=True, stop=True).then_inc(heads_mixed, 1)

            def first_scores(b, n0):
                pe.wait_ge(low_parts, 2 * NCH * b + 2 * NCH)
                pe.wait_ge(v_stored, NCH * b + NCH)
                if not (isinstance(n0, int) and n0 == 0):
                    pe.wait_ge(heads_copied, n0)
                for k in range(KT):
                    scores(n0, 0, k, first=True)
                pe.wait_ge(maxima_joined, b + 1)
                turn_max(n0)
                for k in range(SB):
                    scores(n0 + 1, 1, k, second=True)
                pe.wait_ge(scores_copied, KT * n0 + KT)
                spread_max(n0)

            def ln_center(k, m, src, ready):
                pe.wait_ge(ready, m + 1)
                if k == 0 and not (isinstance(m, int) and m < 2):
                    pe.wait_ge(normed[1], m - 1)
                mm(ps0[:, :], center[:, :], src, start=True, stop=True).then_inc(centered[k], 1)

            def ln_variance(k, m):
                pe.wait_ge(squared[k], m + 1)
                for u in range(4):
                    last = mm(ps0[:, u:u + 1], sq[:, u * P:(u + 1) * P], meancol[:, :], start=True, stop=True)
                last.then_inc(var_ready[k], 1)

            def ln_spread_rsqrt(k, m):
                pe.wait_ge(ln_diag[k], m + 1)
                mm(ps0[:, :], ones[:, :], dgn[:, :, :].rearrange("p a n -> p (a n)"), start=True,
                   stop=True).then_inc(ln_spread[k], 1)

            def l1_queries(m):
                pe.wait_ge(normed[0], m + 1)
                mm(ps0[:, :], wq1_s[:, :], y[:, :], start=True, stop=True).then_inc(l1_q_made, 1)

            def l1_keys_values(m, i):
                pe.wait_ge(l1_q_stored, m + 1)
                if i:
                    pe.wait_ge(l1_kv_stored, 2 * m + 1)
                for u in range(2):
                    last = mm(ps0[:, 2 * u * P:2 * (u + 1) * P], y[:, (2 * i + u) * P:(2 * i + u + 1) * P],
                              wkv1_s[:, :], start=True, stop=True)
                last.then_inc(l1_kv_made, 1)

            def l1_block(m, i):
                pe.wait_ge(edges_masked, m + 1)
                if i:
                    pe.wait_ge(window_added, 4 * m + 2)
                for u in range(2):
                    last = mm(ps0[:, 0:3 * P], k3[:, 2 * i + u, :],
                              v3[:, 2 * i + u, :, :].rearrange("p a n -> p (a n)"), start=(u == 0), stop=(u == 1))
                last.then_inc(block_summed, 1)

            def l1_attend(m, par):
                pe.wait_ge(window_scaled, m + 1)
                pe.wait_ge(l1_q_stored, m + 1)
                for i in range(2):
                    last = mm(ps0[:, 2 * i * P:2 * (i + 1) * P], mcur[:, i, :], q1[:, par, 2 * i * P:2 * (i + 1) * P],
                              start=True, stop=True)
                last.then_inc(attended, 1)

            def router(m):
                pe.wait_ge(normed[1], m + 1)
                pe.wait_ge(heads_normed, min(m + LAG, B * NCH) if isinstance(m, int) else m + LAG)
                for u in range(4):
                    last = mm(ps2[:, u * E:(u + 1) * E], z[:, u * P:(u + 1) * P], rw_s[:, :], start=True, stop=True)
                last.then_inc(logits_made, 1)

            def turn_gates(m):
                pe.wait_ge(gate_step, GATE_STEPS * m + GATE_STEPS)
                dst = ps2[0:GROWS, 0:T // 2].bitcast(bf16)
                for u in range(4):
                    last = nc.tensor.transpose(dst[:, u * P:(u + 1) * P], gparts[:, u, :], identb[:, :])
                last.then_inc(gates_turned, 1)

            def expert_bias(m):
                pe.wait_ge(gates_stored, m + 1)
                mm(ps1[:, :], eb_s[:, :], gT[:, :], start=True, stop=False)

            def spread_gate(m, e):
                if e:
                    pe.wait_ge(gated, E * m + e)
                mm(ps2[:, :], sel[:, e, :], gT[0:E * GPARTS, :], start=True, stop=True).then_inc(gate_spread, 1)

            def expert(m, e):
                pe.wait_ge(gated, E * m + e + 1)
                mm(ps1[:, :], ew_s[:, e, :], zg[:, e % 2, :], start=False, stop=(e == E - 1)).then_inc(expert_done, 1)

            def heads(n, j):
                if has(n, 1):
                    if j == 0:
                        spread_sums(n - 1)
                    if j == 1:
                        mix_heads(n - 1)

            def side(n, c, par, j):
                if has(n, 3):
                    if j == 1:
                        ln_spread_rsqrt(1, n - 3)
                    if j == 2:
                        router(n - 3)
                    if j == GATE_STEP:
                        expert_bias(n - 3)
                    if GATE_STEP <= j < GATE_STEP + E:
                        spread_gate(n - 3, j - GATE_STEP)
                    if GATE_STEP < j < GATE_STEP + E:
                        expert(n - 3, j - GATE_STEP - 1)
                if has(n, 4) and j == -1:
                    expert(n - 4, E - 1)
                if has(n, 1):
                    if j == 2:
                        ln_center(0, n - 1, tt[:, 1 - par, :], layer0_out)
                    if j == 3:
                        ln_variance(0, n - 1)
                    if j == 5:
                        ln_spread_rsqrt(0, n - 1)
                    if j == 6:
                        l1_queries(n - 1)
                    if j in (7, 8):
                        l1_keys_values(n - 1, j - 7)
                    if j in (10, 11):
                        l1_block(n - 1, j - 10)
                if has(n, 3) and j == GATE_STEP - 2:
                    turn_gates(n - 3)
                if has(n, 2):
                    if j == attend_step(n):
                        l1_attend(n - 2, par)
                    if j == attend_step(n) + 1:
                        ln_center(1, n - 2, t1[:, par, :], t1_ready)
                    if j == attend_step(n) + 2:
                        ln_variance(1, n - 2)

            def chunk(b, c, n, par, ahead, stage):
                side(n, c, par, -1)
                side(n, c, par, 0)
                for j in range(NP):
                    if j < NP - 1:
                        values(n, j)
                    heads(n, j)
                    if ahead:
                        for k in (2 * j, 2 * j + 1):
                            if k >= SB:
                                scores(n + 1, c + 1, k)
                    if j == NP - 1:
                        values(n, j)
                    if j:
                        side(n, c, par, j)
                    if stage == "statistics" and j == NP - 1:
                        group_statistics(b + 1, n)
                    if stage == "project":
                        if j % 2 == 0:
                            project_keys_queries(b + 1, j // 2)
                        else:
                            project_values(b + 1, j // 2)
                if ahead:
                    turn_max(n + 1)
                if ahead == 2:
                    for k in range(SB):
                        scores(n + 2, c + 2, k)
                if ahead:
                    spread_max(n + 1)
                if stage == "statistics":
                    pe.wait_ge(prep_step, PREP_STEPS * (b + 1) + NCH + 3)
                sum_rows(n)

            def drain(n, c, par, j):
                heads(n, j)
                side(n, c, par, j)

            walk(pe, prepare, first_scores, chunk, drain)


def kernel(**inputs):
    import numpy as np
    import concourse.bacc as bacc
    from concourse.bass_utils import run_bass_kernel_spmd

    def arr(name):
        return np.ascontiguousarray(inputs[name])

    def col(name):
        return arr(name).reshape(-1, 1)

    def rows(a, n=128):
        return np.ascontiguousarray(np.broadcast_to(a.reshape(1, -1), (n, a.size)))

    x = arr("x")
    b, c, hh, ww = x.shape
    e = inputs["L1_ffn_router_w"].shape[1]
    f = np.float32
    group = np.zeros((c, c), f)
    for g in range(0, c, 4):
        group[g:g + 4, g:g + 4] = 0.25
    center = np.full((c, c), -1.0 / c, f)
    center[np.arange(c), np.arange(c)] = 1.0 - 1.0 / c
    sel = np.zeros((3 * e, e * 128), f)
    lower = np.zeros((e, e), f)
    for i in range(e):
        for part in range(3):
            sel[part * e + i, i * 128:(i + 1) * 128] = 1.0
        lower[i, :i] = 1.0
    edges = np.ones((128, 2, 4), f)
    edges[127, 0, 1::2] = 0.0
    edges[0, 1, 0::2] = 0.0
    w1 = "L1_attn_W"
    arrays = {
        "x_in": x.reshape(b, c, hh * ww),
        "norm_w": col("L0_conv_norm_w"), "norm_b": col("L0_conv_norm_b"),
        "wq": arr("L0_conv_Wq"), "bq": col("L0_conv_bq"),
        "wk": arr("L0_conv_Wk"), "bk": col("L0_conv_bk"),
        "wv": arr("L0_conv_Wv"), "bv_rows": rows(arr("L0_conv_bv")),
        "wo": arr("L0_conv_Wo"), "bo": col("L0_conv_bo"),
        "l1_wqT": np.ascontiguousarray(arr(w1 + "q").T), "l1_bq": col("L1_attn_bq"),
        "l1_wkvT": np.ascontiguousarray(np.concatenate([arr(w1 + "k").T, arr(w1 + "v").T], axis=1)),
        "l1_bkv_rows": rows(np.concatenate([arr("L1_attn_bk"), arr("L1_attn_bv")])),
        "router_w": arr("L1_ffn_router_w"), "router_b_rows": rows(arr("L1_ffn_router_b")),
        "expert_w": arr("L1_ffn_expert_w"),
        "expert_b9": np.tile(np.concatenate([np.tile(arr("L1_ffn_expert_b"), (3, 1)), np.zeros((8, 128), f)]), (3, 1)),
        "c_ident": np.eye(128, dtype=f), "c_center": center,
        "c_mean": np.full((128, 1), 1.0 / c, f), "c_group": group,
        "c_sel": sel, "c_lower": rows(lower), "c_edges": edges.reshape(128, 8),
    }
    nc = bacc.Bacc("TRN2", target_bir_lowering=False, num_devices=1)
    args = [nc.dram_tensor(n, a.shape, mybir.dt.float32, kind="ExternalInput").ap() for n, a in arrays.items()]
    args.append(nc.dram_tensor("out", (b, c, hh * ww), mybir.dt.float32, kind="ExternalOutput").ap())
    conv_attn_hybrid_kernel(nc, *args)
    r = run_bass_kernel_spmd(nc, [arrays], core_ids=[0])
    return r.results[0]["out"].reshape(b, c, hh, ww)
```
